# Optimizing a Trainium2 kernel written in Bass

```python
import numpy as np
import jax
import jax.numpy as jnp

def _softmax(x, axis=-1):
    return jax.nn.softmax(x, axis=axis)

def _gelu(x):
    return jax.nn.gelu(x, approximate=True)

def _silu(x):
    return jax.nn.silu(x)

def _sigmoid(x):
    return jax.nn.sigmoid(x)

def _layernorm(x, axis=-1, eps=1e-05):
    m = jnp.mean(x, axis=axis, keepdims=True)
    v = jnp.var(x, axis=axis, keepdims=True)
    return (x - m) / jnp.sqrt(v + eps)

def _scatter_add(tgt, idx, src, axis=0):
    return tgt.at[idx].add(src)

def _segment_sum(src, seg, n):
    return jax.ops.segment_sum(src, seg, n)
kernel_name = 'mk_gnn_resnorm_d4_gnn_r32_58850a'

def setup_inputs(seed: int=0):
    np.random.seed(seed)
    _w = jnp.asarray

    def _rec_inputs():
        import jax
        import jax.numpy as jnp
        _gk = jax.random.key(seed)
        x = -0.0003713 + 1 * jax.random.normal(jax.random.fold_in(_gk, 1), (50000, 128), jnp.float32)
        src = jax.random.randint(jax.random.fold_in(_gk, 2), (50000,), 0, 50000, jnp.int32)
        dst = jnp.minimum((50000 * jax.random.uniform(jax.random.fold_in(_gk, 3), (50000,)) ** 2.0).astype(jnp.int32), 49999)
        _o = jnp.argsort(dst, stable=True)
        src = src[_o]
        dst = dst[_o]
        edge_attr_128 = -6.74381e-05 + 0.999835 * jax.random.normal(jax.random.fold_in(_gk, 12), (50000, 128), jnp.float32)
        edge_attr_8 = jax.random.uniform(jax.random.fold_in(_gk, 13), (50000, 8), jnp.float32, 0.0, 1)
        edge_weight1 = 0.00121237 + 1.00026 * jax.random.normal(jax.random.fold_in(_gk, 15), (50000, 1), jnp.float32)
        return (x, src, dst, edge_attr_128, edge_attr_8, edge_weight1)
    x, src, dst, edge_attr_128, edge_attr_8, edge_weight1 = _rec_inputs()

    def _L0_gnn_setup():
        import jax, jax.numpy as jnp
        import numpy as np
        N, E = (3125, 50000)
        NODE_DIM, EDGE_DIM, NUM_BASIS, LMAX = (128, 128, 8, 0)
        NUM_SH = (LMAX + 1) ** 2
        key = jax.random.key(seed)
        ks = jax.random.split(key, 12)
        inp = {'node_feats': jax.random.normal(ks[0], (N, NODE_DIM), dtype=jnp.float32), 'edge_index': jax.random.randint(ks[1], (2, E), 0, N, dtype=jnp.int64), 'edge_rbf': jax.random.uniform(ks[2], (E, NUM_BASIS), dtype=jnp.float32), 'edge_sh': jax.random.normal(ks[3], (E, NUM_SH), dtype=jnp.float32), 'W1': jax.random.normal(ks[4], (NUM_BASIS, EDGE_DIM), dtype=jnp.float32) / np.sqrt(NUM_BASIS), 'b1': jnp.zeros((EDGE_DIM,), dtype=jnp.float32), 'W2': jax.random.normal(ks[5], (EDGE_DIM, NODE_DIM * (LMAX + 1)), dtype=jnp.float32) / np.sqrt(EDGE_DIM), 'b2': jnp.zeros((NODE_DIM * (LMAX + 1),), dtype=jnp.float32), 'Wself': jax.random.normal(ks[6], (NODE_DIM, NODE_DIM), dtype=jnp.float32) / np.sqrt(NODE_DIM), 'bself': jnp.zeros((NODE_DIM,), dtype=jnp.float32), 'Wcat': jax.random.normal(ks[7], (2 * NODE_DIM, NODE_DIM), dtype=jnp.float32) / np.sqrt(2 * NODE_DIM), 'bcat': jnp.zeros((NODE_DIM,), dtype=jnp.float32)}
        return inp
    _L0_gnn_all = _L0_gnn_setup()
    _L0_gnn_in = {k: v for k, v in _L0_gnn_all.items() if k in ('W1', 'b1', 'W2', 'b2', 'Wself', 'bself', 'Wcat', 'bcat')}
    del _L0_gnn_all

    def _L1_gnn_setup():
        import jax, jax.numpy as jnp
        import numpy as np
        N, E, D, L = (50000, 625000, 128, 2)
        NEG_SLOPE = 0.01

        def _segment_softmax(e, seg, num_segments):
            m = jax.ops.segment_max(e, seg, num_segments=num_segments)
            ex = jnp.exp(e - m[seg])
            s = jax.ops.segment_sum(ex, seg, num_segments=num_segments)
            return ex / s[seg]
        key = jax.random.key(seed)
        ks = jax.random.split(key, 8)
        s = 1.0 / np.sqrt(D)
        return {'x': jax.random.normal(ks[0], (N, D), jnp.float32), 'r_h': jax.random.normal(ks[1], (E, D), jnp.float32), 'src': jax.random.randint(ks[2], (E,), 0, N), 'dst': jax.random.randint(ks[3], (E,), 0, N), 'W': jax.random.normal(ks[4], (L, D, D), jnp.float32) * s, 'Wr': jax.random.normal(ks[5], (L, D, D), jnp.float32) * s, 'Att': jax.random.normal(ks[6], (L, 3 * D), jnp.float32) * s, 'Loop': jax.random.normal(ks[7], (L, D, D), jnp.float32) * s}
    _L1_gnn_all = _L1_gnn_setup()
    _L1_gnn_in = {k: v for k, v in _L1_gnn_all.items() if k in ('W', 'Wr', 'Att', 'Loop')}
    del _L1_gnn_all

    def _L2_gnn_setup():
        import jax, jax.numpy as jnp
        import numpy as np
        N = 3125
        E = 50000
        HID = 128
        H = 8
        D = HID // H
        SCALING = D ** (-0.5)
        key = jax.random.key(seed)
        ks = jax.random.split(key, 12)
        h = jax.random.normal(ks[0], (N, HID), dtype=jnp.float32)
        row = jax.random.randint(ks[1], (E,), 0, N, dtype=jnp.int64)
        col = jax.random.randint(ks[2], (E,), 0, N, dtype=jnp.int64)
        s = 1.0 / np.sqrt(HID)
        Wq = jax.random.uniform(ks[3], (HID, HID), jnp.float32, -s, s)
        bq = jax.random.uniform(ks[4], (HID,), jnp.float32, -s, s)
        Wk = jax.random.uniform(ks[5], (HID, HID), jnp.float32, -s, s)
        bk = jax.random.uniform(ks[6], (HID,), jnp.float32, -s, s)
        Wv = jax.random.uniform(ks[7], (HID, HID), jnp.float32, -s, s)
        bv = jax.random.uniform(ks[8], (HID,), jnp.float32, -s, s)
        Wo = jax.random.uniform(ks[9], (HID, HID), jnp.float32, -s, s)
        bo = jax.random.uniform(ks[10], (HID,), jnp.float32, -s, s)
        return {'h': h, 'row': row, 'col': col, 'Wq': Wq, 'bq': bq, 'Wk': Wk, 'bk': bk, 'Wv': Wv, 'bv': bv, 'Wo': Wo, 'bo': bo}
    _L2_gnn_all = _L2_gnn_setup()
    _L2_gnn_in = {k: v for k, v in _L2_gnn_all.items() if k in ('Wq', 'bq', 'Wk', 'bk', 'Wv', 'bv', 'Wo', 'bo')}
    del _L2_gnn_all

    def _L3_gnn_setup():
        import jax, jax.numpy as jnp
        import numpy as np
        N_LAYERS = 5
        BN_EPS = 1e-05

        def _bn(h, g, b):
            m = h.mean(axis=0)
            v = h.var(axis=0)
            return (h - m) * jax.lax.rsqrt(v + BN_EPS) * g + b
        key = jax.random.key(seed)
        ks = jax.random.split(key, 12)
        N, E, D = (3125, 18750, 128)
        x = jax.random.normal(ks[0], (N, D), dtype=jnp.float32)
        edge_index = jax.random.randint(ks[1], (2, E), 0, N, dtype=jnp.int32)
        s = 1.0 / np.sqrt(D)
        W1 = jax.random.uniform(ks[2], (N_LAYERS, D, D), jnp.float32, -s, s)
        b1 = jax.random.uniform(ks[3], (N_LAYERS, D), jnp.float32, -s, s)
        W2 = jax.random.uniform(ks[4], (N_LAYERS, D, D), jnp.float32, -s, s)
        b2 = jax.random.uniform(ks[5], (N_LAYERS, D), jnp.float32, -s, s)
        g1 = jnp.ones((N_LAYERS, D), jnp.float32)
        beta1 = jnp.zeros((N_LAYERS, D), jnp.float32)
        g2 = jnp.ones((N_LAYERS, D), jnp.float32)
        beta2 = jnp.zeros((N_LAYERS, D), jnp.float32)
        eps = jnp.zeros((N_LAYERS,), jnp.float32)
        return {'x': x, 'edge_index': edge_index, 'W1': W1, 'b1': b1, 'W2': W2, 'b2': b2, 'g1': g1, 'beta1': beta1, 'g2': g2, 'beta2': beta2, 'eps': eps}
    _L3_gnn_all = _L3_gnn_setup()
    _L3_gnn_in = {k: v for k, v in _L3_gnn_all.items() if k in ('W1', 'b1', 'W2', 'b2', 'g1', 'beta1', 'g2', 'beta2', 'eps')}
    del _L3_gnn_all
    return {'x': x, 'src': src, 'dst': dst, 'edge_attr_128': edge_attr_128, 'edge_attr_8': edge_attr_8, 'edge_weight1': edge_weight1, 'L0_gnn_W1': _L0_gnn_in['W1'], 'L0_gnn_b1': _L0_gnn_in['b1'], 'L0_gnn_W2': _L0_gnn_in['W2'], 'L0_gnn_b2': _L0_gnn_in['b2'], 'L0_gnn_Wself': _L0_gnn_in['Wself'], 'L0_gnn_bself': _L0_gnn_in['bself'], 'L0_gnn_Wcat': _L0_gnn_in['Wcat'], 'L0_gnn_bcat': _L0_gnn_in['bcat'], 'L1_gnn_W': _L1_gnn_in['W'], 'L1_gnn_Wr': _L1_gnn_in['Wr'], 'L1_gnn_Att': _L1_gnn_in['Att'], 'L1_gnn_Loop': _L1_gnn_in['Loop'], 'L2_gnn_Wq': _L2_gnn_in['Wq'], 'L2_gnn_bq': _L2_gnn_in['bq'], 'L2_gnn_Wk': _L2_gnn_in['Wk'], 'L2_gnn_bk': _L2_gnn_in['bk'], 'L2_gnn_Wv': _L2_gnn_in['Wv'], 'L2_gnn_bv': _L2_gnn_in['bv'], 'L2_gnn_Wo': _L2_gnn_in['Wo'], 'L2_gnn_bo': _L2_gnn_in['bo'], 'L3_gnn_W1': _L3_gnn_in['W1'], 'L3_gnn_b1': _L3_gnn_in['b1'], 'L3_gnn_W2': _L3_gnn_in['W2'], 'L3_gnn_b2': _L3_gnn_in['b2'], 'L3_gnn_g1': _L3_gnn_in['g1'], 'L3_gnn_beta1': _L3_gnn_in['beta1'], 'L3_gnn_g2': _L3_gnn_in['g2'], 'L3_gnn_beta2': _L3_gnn_in['beta2'], 'L3_gnn_eps': _L3_gnn_in['eps']}

def reference(x, src, dst, edge_attr_128, edge_attr_8, edge_weight1, L0_gnn_W1, L0_gnn_b1, L0_gnn_W2, L0_gnn_b2, L0_gnn_Wself, L0_gnn_bself, L0_gnn_Wcat, L0_gnn_bcat, L1_gnn_W, L1_gnn_Wr, L1_gnn_Att, L1_gnn_Loop, L2_gnn_Wq, L2_gnn_bq, L2_gnn_Wk, L2_gnn_bk, L2_gnn_Wv, L2_gnn_bv, L2_gnn_Wo, L2_gnn_bo, L3_gnn_W1, L3_gnn_b1, L3_gnn_W2, L3_gnn_b2, L3_gnn_g1, L3_gnn_beta1, L3_gnn_g2, L3_gnn_beta2, L3_gnn_eps):
    import jax
    import jax.numpy as jnp

    def _L0_gnn_ref(node_feats, edge_index, edge_rbf, edge_sh, W1, b1, W2, b2, Wself, bself, Wcat, bcat):
        import jax, jax.numpy as jnp
        import numpy as np
        N, E = (3125, 50000)
        NODE_DIM, EDGE_DIM, NUM_BASIS, LMAX = (128, 128, 8, 0)
        NUM_SH = (LMAX + 1) ** 2
        row, col = (edge_index[0], edge_index[1])
        n_nodes = node_feats.shape[0]
        h = jax.nn.silu(edge_rbf @ W1 + b1)
        weights = (h @ W2 + b2).reshape(-1, NODE_DIM, LMAX + 1)
        node_j = node_feats[col]
        messages = (node_j[:, :, None] * weights).sum(axis=-1)
        aggregated = jax.ops.segment_sum(messages, row, num_segments=n_nodes)
        self_out = node_feats @ Wself + bself
        combined = jnp.concatenate([self_out, aggregated], axis=-1)
        return combined @ Wcat + bcat

    def _L1_gnn_ref(x, r_h, src, dst, W, Wr, Att, Loop):
        import jax, jax.numpy as jnp
        import numpy as np
        N, E, D, L = (50000, 625000, 128, 2)
        NEG_SLOPE = 0.01

        def _segment_softmax(e, seg, num_segments):
            m = jax.ops.segment_max(e, seg, num_segments=num_segments)
            ex = jnp.exp(e - m[seg])
            s = jax.ops.segment_sum(ex, seg, num_segments=num_segments)
            return ex / s[seg]
        n = x.shape[0]
        h = x
        for l in range(W.shape[0]):
            hh = h @ W[l]
            rh = r_h @ Wr[l]
            hs = hh[src]
            a = Att[l]
            d = hh.shape[1]
            e = hs @ a[:d] + (hh @ a[d:2 * d])[dst] + rh @ a[2 * d:]
            e = jnp.where(e > 0, e, NEG_SLOPE * e)
            alpha = _segment_softmax(e, dst, n)
            msg = alpha[:, None] * (hs + rh)
            agg = jax.ops.segment_sum(msg, dst, num_segments=n)
            h = jax.nn.relu(agg + hh @ Loop[l])
        return h

    def _L2_gnn_ref(h, row, col, Wq, bq, Wk, bk, Wv, bv, Wo, bo):
        import jax, jax.numpy as jnp
        import numpy as np
        N = 3125
        E = 50000
        HID = 128
        H = 8
        D = HID // H
        SCALING = D ** (-0.5)
        n = h.shape[0]
        q = (h @ Wq.T + bq).reshape(n, D, H) * SCALING
        k = (h @ Wk.T + bk).reshape(n, D, H)
        v = (h @ Wv.T + bv).reshape(n, D, H)
        logits = jnp.einsum('edh,edh->eh', q[row], k[col])
        m = jax.ops.segment_max(logits, row, num_segments=n)
        m = jnp.where(jnp.isfinite(m), m, 0.0)
        ex = jnp.exp(logits - m[row])
        s = jax.ops.segment_sum(ex, row, num_segments=n)
        attn = ex / jnp.where(s[row] == 0, 1.0, s[row])
        out = jax.ops.segment_sum(attn[:, None, :] * v[col], row, num_segments=n)
        return out.reshape(n, -1) @ Wo.T + bo

    def _L3_gnn_ref(x, edge_index, W1, b1, W2, b2, g1, beta1, g2, beta2, eps):
        import jax, jax.numpy as jnp
        import numpy as np
        N_LAYERS = 5
        BN_EPS = 1e-05

        def _bn(h, g, b):
            m = h.mean(axis=0)
            v = h.var(axis=0)
            return (h - m) * jax.lax.rsqrt(v + BN_EPS) * g + b
        N = x.shape[0]
        row, col = (edge_index[0], edge_index[1])
        h = x
        for l in range(N_LAYERS):
            neighbor_sum = jax.ops.segment_sum(h[col], row, num_segments=N)
            h_agg = (1.0 + eps[l]) * h + neighbor_sum
            t = jax.nn.relu(_bn(h_agg @ W1[l] + b1[l], g1[l], beta1[l]))
            t = t @ W2[l] + b2[l]
            h = jax.nn.relu(_bn(t, g2[l], beta2[l]))
        return h
    edge_index = jnp.stack([src, dst])
    x = _layernorm(x + _L0_gnn_ref(x, edge_index, edge_attr_8, edge_weight1, L0_gnn_W1, L0_gnn_b1, L0_gnn_W2, L0_gnn_b2, L0_gnn_Wself, L0_gnn_bself, L0_gnn_Wcat, L0_gnn_bcat), axis=-1)
    x = _layernorm(x + _L1_gnn_ref(x, edge_attr_128, src, dst, L1_gnn_W, L1_gnn_Wr, L1_gnn_Att, L1_gnn_Loop), axis=-1)
    x = _layernorm(x + _L2_gnn_ref(x, src, dst, L2_gnn_Wq, L2_gnn_bq, L2_gnn_Wk, L2_gnn_bk, L2_gnn_Wv, L2_gnn_bv, L2_gnn_Wo, L2_gnn_bo), axis=-1)
    x = _layernorm(x + _L3_gnn_ref(x, edge_index, L3_gnn_W1, L3_gnn_b1, L3_gnn_W2, L3_gnn_b2, L3_gnn_g1, L3_gnn_beta1, L3_gnn_g2, L3_gnn_beta2, L3_gnn_eps), axis=-1)
    return x

_drawn_inputs = setup_inputs


def setup_inputs(seed=0):
    import zlib

    import numpy as np

    out = dict(_drawn_inputs(seed))
    spreads = {'L0_gnn_b1': (0.0, 0.1),
     'L0_gnn_b2': (0.0, 0.1),
     'L0_gnn_bself': (0.0, 0.1),
     'L0_gnn_bcat': (0.0, 0.1),
     'L3_gnn_g1': (1.0, 0.2),
     'L3_gnn_beta1': (0.0, 0.1),
     'L3_gnn_g2': (1.0, 0.2),
     'L3_gnn_beta2': (0.0, 0.1),
     'L3_gnn_eps': (0.0, 0.1)}
    factors = {'L2_gnn_bq': 8.0, 'L2_gnn_bk': 8.0, 'L3_gnn_b1': 8.0, 'L3_gnn_b2': 8.0}
    for name, (base, spread) in spreads.items():
        noise = np.random.default_rng([zlib.crc32(name.encode()), seed]).standard_normal(out[name].shape)
        drawn = base * np.exp(spread * noise) if base else spread * noise
        out[name] = jnp.asarray(drawn.astype(out[name].dtype))
    for name, factor in factors.items():
        out[name] = (out[name] * factor).astype(out[name].dtype)
    return out
```

```python
from contextlib import ExitStack

import concourse.bass as bass
from concourse import mybir

F32 = mybir.dt.float32
I32 = mybir.dt.int32
BF16 = mybir.dt.bfloat16
ALU = mybir.AluOpType
ACT = mybir.ActivationFunctionType

N = 50000
E = 50000
D = 128
P = 128
ET = 392
EP = ET * P
CH = 512
NCH = EP // CH
NS = 256
SUP = (N + NS - 1) // NS
OP = 125
OT = E // OP
PADK = 1.0e6
HI = ET
SW = 16
DW = 132
HEADS = 8
EPS = 1e-5


def ds(i, n):
    return bass.ds(i, n)


class Phase:

    def __init__(self, nc, *names):
        self.nc, self.names = nc, names
        self.stack = ExitStack()

    def __enter__(self):
        self.sems = [self.stack.enter_context(self.nc.semaphore(n)) for n in self.names]
        return self.sems

    def __exit__(self, *a):
        if a[0] is None:
            self.nc.gpsimd.dma_reset()
            for s in self.sems:
                self.nc.gpsimd.sem_clear(s)
            self.nc.all_engine_barrier()
        self.stack.close()


class Chain:

    def __init__(self, eng, sem, base=0):
        self.eng, self.sem, self.base, self.n = eng, sem, base, 0

    def add(self, ins):
        ins.then_inc(self.sem, 1)
        self.n += 1
        return self.n

    def link(self, ins):
        self.add(ins)
        self.eng.wait_ge(self.sem, self.base + self.n)


def setup_constants(nc, S):
    with Phase(nc, "iotas_done", "chain") as (iotas_done, chain):
        with nc.Block() as block:
            @block.gpsimd
            def _(pool):
                nc.gpsimd.iota(S.iota_row[:, :], [[1, HI]], base=0, channel_multiplier=0,
                               allow_small_or_imprecise_dtypes=True).then_inc(iotas_done, 1)
                nc.gpsimd.iota(S.iota_col[:, :], [[0, 1]], base=0, channel_multiplier=1,
                               allow_small_or_imprecise_dtypes=True).then_inc(iotas_done, 1)

            @block.vector
            def _(dve):
                dve.wait_ge(iotas_done, 2)
                c = Chain(dve, chain)
                row, col = S.iota_row[:, 0:P], S.iota_col[:, 0:1]
                c.add(nc.vector.tensor_scalar(S.ident[:, :], row, col, None, ALU.is_equal))
                c.add(nc.vector.tensor_scalar(S.earlier[:, :], row, col, None, ALU.is_lt))
                c.add(nc.vector.tensor_scalar(S.later[:, :], row, col, None, ALU.is_gt))
                c.add(nc.vector.memset(S.ones[:, :], 1.0))
                c.add(nc.vector.memset(S.zeros_bf[:, :], 0.0))
                c.add(nc.vector.tensor_scalar(S.group_base[:, :], S.iota_row[:, 0:SUP], float(NS), None, ALU.mult))


def load_keys(nc, S, src, dst):
    with Phase(nc, "keys_in", "chain") as (keys_in, chain):
        with nc.Block() as block:
            @block.sync
            def _(sp):
                for k, key in enumerate((src, dst)):
                    sp.dma_start(S.key_i[0:OP, k, :], key.rearrange("(p t) -> p t", p=OP)).then_inc(keys_in, 16)

            @block.vector
            def _(dve):
                dve.wait_ge(keys_in, 32)
                c = Chain(dve, chain)
                c.add(nc.vector.tensor_copy(S.key_f[0:OP], S.key_i[0:OP]))
                c.link(nc.vector.tensor_scalar(S.part_i[0:OP], S.key_i[0:OP], 7, None, ALU.logical_shift_right))
                c.link(nc.vector.tensor_copy(S.key_hi[0:OP], S.part_i[0:OP]))
                c.link(nc.vector.tensor_scalar(S.part_i[0:OP], S.key_i[0:OP], 127, None, ALU.bitwise_and))
                c.add(nc.vector.tensor_copy(S.key_lo[0:OP], S.part_i[0:OP]))


def count_keys(nc, S, k):
    with ExitStack() as st:
        hist = st.enter_context(nc.psum_tensor(f"hist{k}", [P, 512], F32))
        with Phase(nc, "onehots_ready", "onehots_used", "hist_done", "start_ready") as (
                onehots_ready, onehots_used, hist_done, start_ready):
            with nc.Block() as block:
                @block.vector
                def _(dve):
                    nc.vector.sem_inc(onehots_used, 2)
                    with dve.Fori(0, OT // 2) as i:
                        for u in range(2):
                            dve.wait_ge(onehots_used, 2 * i + (u + 1))
                            nc.vector.tensor_scalar(S.oh_hi[0:OP, u, :], S.iota_row[0:OP, :],
                                                    S.key_hi[0:OP, k, ds(2 * i + u, 1)], None,
                                                    ALU.is_equal).then_inc(onehots_ready, 1)
                            nc.vector.tensor_scalar(S.oh_lo[0:OP, u, :], S.iota_row[0:OP, 0:P],
                                                    S.key_lo[0:OP, k, ds(2 * i + u, 1)], None,
                                                    ALU.is_equal).then_inc(onehots_ready, 1)
                    dve.wait_ge(hist_done, 1)
                    nc.vector.tensor_copy(S.hist[:, :], hist[:, 0:HI])

                @block.tensor
                def _(pe):
                    nc.tensor.matmul(hist[:, 0:HI], S.zeros_bf[:, 0:P], S.zeros_bf[:, 0:HI], start=True, stop=False)
                    with pe.Fori(0, OT // 2) as i:
                        for u in range(2):
                            pe.wait_ge(onehots_ready, 4 * i + 2 * (u + 1))
                            nc.tensor.matmul(hist[:, 0:HI], S.oh_lo[0:OP, u, :], S.oh_hi[0:OP, u, :],
                                             start=False, stop=False).then_inc(onehots_used, 1)
                    nc.tensor.matmul(hist[:, 0:HI], S.zeros_bf[:, 0:P], S.zeros_bf[:, 0:HI],
                                     start=False, stop=True).then_inc(hist_done, 1)


def start_offsets(nc, S, k):
    with ExitStack() as st:
        below = st.enter_context(nc.psum_tensor(f"below{k}", [P, 512], F32))
        total = st.enter_context(nc.psum_tensor(f"total{k}", [P, 512], F32))
        with Phase(nc, "sums_done", "chain") as (sums_done, chain):
            with nc.Block() as block:
                @block.tensor
                def _(pe):
                    nc.tensor.matmul(below[:, 0:HI], S.later[:, :], S.hist[:, :], start=True, stop=True).then_inc(sums_done, 1)
                    nc.tensor.matmul(total[:, 0:HI], S.ones[:, 0:P], S.hist[:, :], start=True, stop=True).then_inc(sums_done, 1)

                @block.vector
                def _(dve):
                    dve.wait_ge(sums_done, 2)
                    c = Chain(dve, chain)
                    c.link(nc.vector.tensor_copy(S.t392[:, 0, :], total[:, 0:HI]))
                    c.link(nc.vector.tensor_tensor_scan(S.t392[:, 1, :], S.ones[:, 0:HI], S.t392[:, 0, :], 0.0, ALU.mult, ALU.add))
                    c.link(nc.vector.tensor_tensor(S.t392[:, 1, :], S.t392[:, 1, :], S.t392[:, 0, :], ALU.subtract))
                    c.link(nc.vector.tensor_tensor(S.start[:, :], S.t392[:, 1, :], below[:, 0:HI], ALU.add))


def rank_keys(nc, S, k):
    with ExitStack() as st:
        table = st.enter_context(nc.psum_tensor(f"table{k}", [P, 512], F32))
        look = [st.enter_context(nc.psum_tensor(f"look{k}{u}", [P, 512], F32)) for u in range(2)]
        rows = [st.enter_context(nc.psum_tensor(f"rows{k}{u}", [P, 512], F32)) for u in range(2)]
        with Phase(nc, "rows_ready", "dve_done", "table_ready", "table_copied", "looked_up", "cols_ready") as (
                rows_ready, dve_done, table_ready, table_copied, looked_up, cols_ready):
            with nc.Block() as block:
                @block.scalar
                def _(act):
                    nc.scalar.sem_inc(looked_up, 2)
                    with act.Fori(0, OT // 2) as i:
                        nc.scalar.copy(S.cols[0:OP, 0, :], S.key_lo[0:OP, k, ds(2 * i, 2)]).then_inc(cols_ready, 1)
                        nc.scalar.copy(S.cols[0:OP, 1, :], S.key_f[0:OP, k, ds(2 * i, 2)]).then_inc(cols_ready, 1)
                        for u in range(2):
                            act.wait_ge(table_ready, 2 * i + (u + 1))
                            act.wait_ge(looked_up, 2 * i + (u + 1))
                            nc.scalar.activation(S.table[:, u, :], table[:, 0:HI], ACT.Copy).then_inc(table_copied, 1)

                @block.vector
                def _(dve):
                    def lookup(i, u):
                        dve.wait_ge(looked_up, 2 * i + (u + 3))
                        nc.vector.scalar_tensor_tensor(S.junk[0:OP, 2 + u, :], S.iota_row[0:OP, :],
                                                       S.key_hi[0:OP, k, ds(2 * i + u, 1)], look[u][0:OP, 0:HI],
                                                       ALU.is_equal, ALU.mult,
                                                       accum_out=S.base[0:OP, ds(2 * i + u, 1)]).then_inc(dve_done, 1)

                    def onehots(i, u):
                        dve.wait_ge(rows_ready, 2 * i + (u + 1))
                        nc.vector.tensor_scalar(S.ohT_lo[:, u, 0:OP], rows[u][:, 0:OP], S.iota_col[:, 0:1], None,
                                                ALU.is_equal).then_inc(dve_done, 1)
                        nc.vector.tensor_scalar(S.oh_hi[0:OP, u, :], S.iota_row[0:OP, :],
                                                S.key_hi[0:OP, k, ds(2 * i + u, 1)], None,
                                                ALU.is_equal).then_inc(dve_done, 1)
                        nc.vector.tensor_scalar(S.oh_lo[0:OP, u, :], S.iota_row[0:OP, 0:P],
                                                S.key_lo[0:OP, k, ds(2 * i + u, 1)], None,
                                                ALU.is_equal).then_inc(dve_done, 1)
                        nc.vector.scalar_tensor_tensor(S.junk[0:OP, u, 0:OP], rows[u][0:OP, P:P + OP],
                                                       S.key_f[0:OP, k, ds(2 * i + u, 1)], S.earlier[0:OP, 0:OP],
                                                       ALU.is_equal, ALU.mult,
                                                       accum_out=S.rank[0:OP, ds(2 * i + u, 1)]).then_inc(dve_done, 1)

                    dve.sem_inc(dve_done, 1)
                    with dve.Fori(0, OT // 2) as i:
                        onehots(i, 0)
                        onehots(i, 1)
                        lookup(i, 0)
                        lookup(i, 1)
                    dve.wait_ge(dve_done, 10 * (OT // 2) + 1)
                    nc.vector.tensor_tensor(S.pos[0:OP, k, :], S.base[0:OP, :], S.rank[0:OP, :], ALU.add)

                @block.tensor
                def _(pe):
                    nc.tensor.matmul(table[:, 0:HI], S.ident[:, :], S.start[:, :], start=True, stop=True).then_inc(table_ready, 1)
                    with pe.Fori(0, OT // 2) as i:
                        for u in range(2):
                            pe.wait_ge(dve_done, 10 * i + 1)
                            pe.wait_ge(cols_ready, 2 * i + 2)
                            nc.tensor.matmul(rows[u][:, 0:OP], S.cols[0:OP, 0, u:u + 1].broadcast_to([OP, P]),
                                             S.ident[0:OP, 0:OP], start=True, stop=True)
                            nc.tensor.matmul(rows[u][0:OP, P:P + OP], S.cols[0:OP, 1, u:u + 1].broadcast_to([OP, OP]),
                                             S.ident[0:OP, 0:OP], start=True, stop=True).then_inc(rows_ready, 1)
                        for u in range(2):
                            pe.wait_ge(dve_done, 10 * i + (4 * u + 5))
                            pe.wait_ge(table_copied, 2 * i + (u + 1))
                            nc.tensor.matmul(table[:, 0:HI], S.oh_lo[0:OP, u, :], S.oh_hi[0:OP, u, :],
                                             start=False, stop=True, skip_group_check=True).then_inc(table_ready, 1)
                            nc.tensor.matmul(look[u][0:OP, 0:HI], S.ohT_lo[:, u, 0:OP], S.table[:, u, :],
                                             start=True, stop=True).then_inc(looked_up, 1)


def scatter_rows(nc, S, k, width, load, out_sorted):
    U = 8
    NB = OT // U
    C = width - 4 if width == DW else 8
    with ExitStack() as st:
        stage = st.enter_context(nc.sbuf_tensor(f"stage{k}", [P, 2, U, width], F32))
        index = st.enter_context(nc.sbuf_tensor(f"index{k}", [P, 2, U], I32))
        pad = st.enter_context(nc.sbuf_tensor(f"pad{k}", [P, width], F32))
        with Phase(nc, "pad_set", "rows_in0", "rows_in1", "row_keys", "stage_clear", "scattered0", "scattered1", "pool_go") as (
                pad_set, rows_in0, rows_in1, row_keys, stage_clear, scattered0, scattered1, pool_go):
            rows_in, scattered = [rows_in0, rows_in1], [scattered0, scattered1]
            PR = (EP - E) // 2
            with nc.Block() as block:
                @block.sync
                def _(sp):
                    sp.wait_ge(stage_clear, 1)
                    with sp.Fori(0, NB // 2) as i:
                        for u in range(2):
                            sp.wait_ge(scattered[u], 16 + 16 * U * i)
                            sp.dma_start(stage[0:OP, u, :, 0:C], load(2 * i + u, U)).then_inc(rows_in[u], 16)

                @block.vector
                def _(dve):
                    nc.vector.memset(stage[:, :, :, :], 0.0).then_inc(stage_clear, 1)
                    nc.vector.memset(pad[:, :], 0.0).then_inc(pad_set, 1)
                    dve.wait_ge(pad_set, 1)
                    nc.vector.memset(pad[:, C + k:C + k + 1], PADK).then_inc(pad_set, 1)
                    dve.wait_ge(stage_clear, 1)
                    with dve.Fori(0, NB // 2) as i:
                        for u in range(2):
                            dve.wait_ge(scattered[u], 16 + 16 * U * i)
                            at = ds((2 * i + u) * U, U)
                            nc.vector.tensor_copy(stage[0:OP, u, :, C], S.key_f[0:OP, 0, at]).then_inc(row_keys, 1)
                            nc.vector.tensor_copy(stage[0:OP, u, :, C + 1], S.key_f[0:OP, 1, at]).then_inc(row_keys, 1)
                            nc.vector.tensor_copy(index[0:OP, u, :], S.pos[0:OP, k, at]).then_inc(row_keys, 1)

                @block.gpsimd
                def _(pool):
                    pool.wait_ge(pad_set, 2)
                    for u in range(2):
                        nc.gpsimd.dma_start(out_sorted[E + u * PR:E + (u + 1) * PR, :], pad[0:PR, :]).then_inc(scattered[u], 16)
                    with pool.Fori(0, NB // 2) as i:
                        for u in range(2):
                            pool.wait_ge(row_keys, 6 * i + 3 * (u + 1))
                            pool.wait_ge(rows_in[u], 16 * (i + 1))
                            nc.gpsimd.sem_inc(pool_go, 1)
                            for j in range(U):
                                nc.gpsimd.indirect_dma_start(
                                    out_sorted[:, :], bass.IndirectOffsetOnAxis(ap=index[0:OP, u, j:j + 1], axis=0),
                                    stage[0:OP, u, j, :], None).then_inc(scattered[u], 16)
                    for u in range(2):
                        pool.wait_ge(scattered[u], 16 + 16 * U * (NB // 2))


def pad_nodes(nc, S, x, x_pad):
    with Phase(nc, "zero_set", "copied") as (zero_set, copied):
        with nc.Block() as block:
            @block.vector
            def _(dve):
                nc.vector.memset(S.ones[0:88, 0:256], 0.0).then_inc(zero_set, 1)
                dve.wait_ge(copied, 32)
                nc.vector.memset(S.ones[0:88, 0:256], 1.0)

            @block.sync
            def _(sp):
                sp.dma_start(x_pad[0:N, :].rearrange("(p a) d -> p (a d)", p=400),
                             x.rearrange("(p a) d -> p (a d)", p=400)).then_inc(copied, 16)
                sp.wait_ge(zero_set, 1)
                sp.dma_start(x_pad[N:EP, :].rearrange("(p a) d -> p (a d)", a=2), S.ones[0:88, 0:256]).then_inc(copied, 16)


def sorted_keys(nc, S, k, sorted_rows, col):
    name = "sd"[k]
    with Phase(nc, "keys_in", "chain") as (keys_in, chain):
        with nc.Block() as block:
            @block.sync
            def _(sp):
                rows = sorted_rows.rearrange("(t p) w -> p t w", p=P)
                for j in range(4):
                    at = slice(j * ET // 4, (j + 1) * ET // 4)
                    sp.dma_start(S.ends[:, at, :], rows[:, at, col:col + 2]).then_inc(keys_in, 16)

            @block.vector
            def _(dve):
                dve.wait_ge(keys_in, 64)
                c = Chain(dve, chain)
                key, other, last = S.key[k], S.other[k], S.last[k]
                c.link(nc.vector.tensor_copy(key[:, :], S.ends[:, :, k]))
                c.link(nc.vector.tensor_copy(other[:, :], S.ends[:, :, 1 - k]))
                c.add(nc.vector.memset(last[:, :], 0))
                c.link(nc.vector.tensor_scalar(S.tile_f[:, :], key[:, :], float(N - 1), None, ALU.min))
                c.link(nc.vector.tensor_copy(S.tile_i[:, :], S.tile_f[:, :]))
                c.link(nc.vector.tensor_copy(S.keyi[k][:, :], S.tile_i[:, :]))
                c.add(nc.vector.tensor_scalar(last[:, 1:ET + 1], S.tile_i[:, :], 8, None, ALU.logical_shift_right))


def aggregate(nc, S, name, k, out_fm, gather=None, dense=None, weights=None, heads=1):
    B = 8
    NI = ET // B
    key, other, last = S.key[k], S.other[k], S.last[k]
    with ExitStack() as st:
        sb = lambda n, s, d=F32: st.enter_context(nc.sbuf_tensor(f"{name}_{n}", s, d))
        rows = sb("rows", [P, B, D]) if gather is not None else None
        flat = sb("flat", [P, B, D]) if dense is not None else None
        prod = sb("prod", [P, B, D]) if (gather is not None and dense is not None) or weights is not None else None
        msg = prod if prod is not None else (rows if rows is not None else flat)
        index = sb("index", [P, 2, B // 2], I32)
        oh_old = sb("oh_old", [P, 4, NS])
        oh_new = sb("oh_new", [P, 4, NS])
        stage = sb("stage", [P, 4, NS])
        sums = st.enter_context(nc.psum_tensor(f"{name}_sums", [P, 4, 512], F32))
        with Phase(nc, "gathered0", "gathered1", "dense_in0", "dense_in1", "index_ready", "pool_go", "prod_ready",
                   "old_ready", "new_ready", "tile_begun", "group_begun", "evacuated",
                   "stored0", "stored1", "stored2", "stored3") as (
                gathered0, gathered1, dense_in0, dense_in1, index_ready, pool_go, prod_ready,
                old_ready, new_ready, tile_begun, group_begun, evacuated, *stored):
            gathered, dense_in = [gathered0, gathered1], [dense_in0, dense_in1]
            with nc.Block() as block:
                @block.sync
                def _(sp):
                    if dense is None:
                        return
                    with sp.Fori(0, NI) as i:
                        for h in range(2):
                            sp.wait_ge(tile_begun, B * i + 4 * h + 1)
                            t0 = B * i + 4 * h
                            sp.dma_start(flat[:, 4 * h:4 * h + 4, :],
                                         dense[ds(t0 * P, 4 * P), 0:D].rearrange("(t p) d -> p t d", p=P)).then_inc(dense_in[h], 16)

                @block.gpsimd
                def _(pool):
                    if gather is not None:
                        with pool.Fori(0, NI) as i:
                            for h in range(2):
                                pool.wait_ge(index_ready, 2 * i + (h + 1))
                                pool.wait_ge(tile_begun, B * i + 4 * h + 1)
                                nc.gpsimd.sem_inc(pool_go, 1)
                                for j in range(4):
                                    nc.gpsimd.indirect_dma_start(
                                        rows[:, 4 * h + j, :], None, gather[:, :],
                                        bass.IndirectOffsetOnAxis(ap=index[:, h, j:j + 1], axis=0)).then_inc(gathered[h], 16)
                        for h in range(2):
                            pool.wait_ge(gathered[h], 64 * NI)
                    if weights is not None:
                        with pool.Fori(0, NI) as i:
                            for h in range(2):
                                pool.wait_ge(dense_in[h], 16 * (i + 1))
                                pool.wait_ge(tile_begun, B * i + 4 * h + 1)
                                nc.gpsimd.sem_inc(pool_go, 1)
                                for j in range(4):
                                    u = 4 * h + j
                                    w = weights[:, ds((B * i + u) * heads, heads)]
                                    nc.gpsimd.tensor_tensor(
                                        prod[:, u, :].rearrange("p (a h) -> p a h", h=heads),
                                        flat[:, u, :].rearrange("p (a h) -> p a h", h=heads),
                                        w.unsqueeze(1).broadcast_to([P, D // heads, heads]),
                                        ALU.mult).then_inc(prod_ready, 1)

                @block.scalar
                def _(act):
                    for u in range(4):
                        act.dma_start(S.scratch[u:u + 1, :], S.ones[0:1, 0:16]).then_inc(stored[u], 16)
                    with act.Fori(0, SUP // 4) as q:
                        for u in range(4):
                            act.wait_ge(stored[u], 16 * q + 16)
                            act.wait_ge(group_begun, 4 * q + u + 5)
                            nc.scalar.copy(stage[:, u, :], sums[:, u, 0:NS]).then_inc(evacuated, 1)
                            act.wait_ge(evacuated, 4 * q + u + 5)
                            act.dma_start(out_fm[:, ds((4 * q + u) * NS, NS)], stage[:, u, :]).then_inc(stored[u], 16)
                    for u in range(4):
                        act.wait_ge(stored[u], 16 * (SUP // 4 + 1))

                @block.vector
                def _(dve):
                    with dve.Fori(0, NI) as i:
                        for u in range(B):
                            h = u // 4
                            t = B * i + u
                            n0 = dve.value_load(last[127:128, ds(t, 1)], min_val=0, max_val=SUP - 1)
                            n1 = dve.value_load(last[127:128, ds(t + 1, 1)], min_val=0, max_val=SUP - 1)
                            if gather is not None and u % 4 == 0:
                                if u == 0:
                                    dve.wait_ge(tile_begun, B * i + 1)
                                dve.wait_ge(tile_begun, B * i + u + 1)
                                nc.vector.tensor_copy(index[:, h, :], S.gidx[k][:, ds(t, 4)]).then_inc(index_ready, 1)
                            if gather is not None and dense is not None:
                                dve.wait_ge(gathered[h], 64 * i + 16 * 4)
                                dve.wait_ge(dense_in[h], 16 * i + 16)
                                dve.wait_ge(tile_begun, B * i + 4 * h + 1)
                                nc.vector.tensor_tensor(prod[:, u, :], rows[:, u, :], flat[:, u, :], ALU.mult).then_inc(prod_ready, 1)
                            dve.wait_ge(tile_begun, t + 1)
                            nc.vector.tensor_scalar(oh_old[:, u % 4, :], S.iota_row[:, 0:NS], S.group_base[:, ds(n0, 1)],
                                                    key[:, ds(t, 1)], ALU.add, ALU.is_equal).then_inc(old_ready, 1)
                            with dve.If(n0 < n1):
                                with dve.Fori(n0 + 1, n1 + 1) as n:
                                    dve.wait_ge(group_begun, n)
                                    nc.vector.tensor_scalar(oh_new[:, ds(n & 3, 1), :].rearrange("p a s -> p (a s)"), S.iota_row[:, 0:NS],
                                                            S.group_base[:, ds(n, 1)], key[:, ds(t, 1)],
                                                            ALU.add, ALU.is_equal).then_inc(new_ready, 1)

                @block.tensor
                def _(pe):
                    pe.sem_inc(tile_begun, 4)
                    pe.sem_inc(group_begun, 4)
                    pe.sem_inc(evacuated, 4)
                    nc.tensor.matmul(sums[:, 0, 0:NS], S.zeros_bf[:, 0:P], S.zeros_bf[:, 0:NS], start=True, stop=True)
                    with pe.Fori(0, NI) as i:
                        for u in range(B):
                            h = u // 4
                            t = B * i + u
                            n0 = pe.value_load(last[127:128, ds(t, 1)], min_val=0, max_val=SUP - 1)
                            n1 = pe.value_load(last[127:128, ds(t + 1, 1)], min_val=0, max_val=SUP - 1)
                            if prod is not None:
                                pe.wait_ge(prod_ready, t + 1)
                            elif gather is not None:
                                pe.wait_ge(gathered[h], 64 * i + 64)
                            else:
                                pe.wait_ge(dense_in[h], 16 * i + 16)
                            pe.wait_ge(old_ready, t + 1)
                            nc.tensor.matmul(sums[:, ds(n0 & 3, 1), 0:NS].rearrange("p a s -> p (a s)"), msg[:, u, :], oh_old[:, u % 4, :],
                                             start=False, stop=True, skip_group_check=True).then_inc(tile_begun, 1)
                            with pe.If(n0 < n1):
                                with pe.Fori(n0 + 1, n1 + 1) as n:
                                    pe.wait_ge(new_ready, n)
                                    pe.wait_ge(evacuated, n + 1)
                                    nc.tensor.matmul(sums[:, ds(n & 3, 1), 0:NS].rearrange("p a s -> p (a s)"), msg[:, u, :],
                                                     oh_new[:, ds(n & 3, 1), :].rearrange("p a s -> p (a s)"),
                                                     start=True, stop=True, skip_group_check=True).then_inc(group_begun, 1)
                    g = (SUP - 1) % 4
                    nc.tensor.matmul(sums[:, g, 0:NS], S.zeros_bf[:, 0:P], S.zeros_bf[:, 0:NS],
                                     start=False, stop=True, skip_group_check=True).then_inc(group_begun, 1)


def gate(eng, passed):
    eng.sem_inc(passed, 1)


def prime(eng, S, sems):
    for n, s in enumerate(sems):
        eng.dma_start(S.scratch[n:n + 1, :], S.ones[0:1, 0:16]).then_inc(s, 16)


def trips(eng, body, peel=False):
    n = NCH // 2
    with eng.Fori(0, n - 1 if peel else n) as i:
        body(i, False)
    if peel:
        body(n - 1, True)


def filter_rows(nc, S, by_src, W1, b1, W2, b2, edge_w):
    with ExitStack() as st:
        sb = lambda n, s, d=F32: st.enter_context(nc.sbuf_tensor(f"f0_{n}", s, d))
        ps = lambda n: [st.enter_context(nc.psum_tensor(f"f0_{n}{u}", [P, 512], F32)) for u in range(2)]
        w1 = sb("w1", [4 * SW, 4, D]); w2 = sb("w2", [D, D]); b1c = sb("b1c", [D, 1]); b2r = sb("b2r", [P, D])
        basis = sb("basis", [P, 2, 4, SW]); basisT = sb("basisT", [4 * SW, 2, P]); hid = sb("hid", [D, 2, 512])
        sig = sb("sig", [D, 2, 512]); lin = sb("lin", [D, 2, 512])
        stage = sb("stage", [P, 2, 4, D])
        turned, hidden, factor = ps("turned"), ps("hidden"), ps("factor")
        with Phase(nc, "w_zero", "w_in", "in0", "in1", "turned_ready", "basisT_ready", "hidden_ready", "act_done", "hid_ready",
                   "factor_ready", "stage_ready", "stored0", "stored1") as (
                w_zero, w_in, in0, in1, turned_ready, basisT_ready, hidden_ready, act_done, hid_ready, factor_ready, stage_ready, stored0, stored1):
            loaded, stored = [in0, in1], [stored0, stored1]
            with nc.Block() as block:
                @block.sync
                def _(sp):
                    sp.wait_ge(w_zero, 1)
                    for j in range(4):
                        sp.dma_start(w1[SW * j:SW * j + 8, j, :], W1).then_inc(w_in, 16)
                    sp.dma_start(w2[:, :], W2).then_inc(w_in, 16)
                    sp.dma_start(b1c[:, :], b1.rearrange("(p o) -> p o", o=1)).then_inc(w_in, 16)
                    sp.dma_start(b2r[:, :], b2.rearrange("(o f) -> o f", o=1).broadcast_to([P, D])).then_inc(w_in, 16)

                    def body(i, tail):
                        for u in range(2):
                            sp.wait_ge(turned_ready, 2 * i + (u + 1))
                            sp.dma_start(basis[:, u, :, :], by_src[ds((2 * i + u) * CH, CH), :].rearrange("(t p) w -> p t w", p=P)).then_inc(loaded[u], 16)
                    trips(sp, body)

                @block.tensor
                def _(pe):
                    pe.wait_ge(w_in, 16 * 7)
                    pe.sem_inc(turned_ready, 2)

                    def body(i, tail):
                        for u in range(2):
                            pe.wait_ge(loaded[u], 16 * i + 16)
                            pe.wait_ge(basisT_ready, 2 * i + (u + 1))
                            nc.tensor.matmul(turned[u][0:4 * SW, 0:P], basis[:, u, :, :].rearrange("p t w -> p (t w)"),
                                             S.ident[:, :], start=True, stop=True).then_inc(turned_ready, 1)
                        for u in range(2):
                            pe.wait_ge(basisT_ready, 2 * i + (u + 3))
                            pe.wait_ge(hid_ready, 2 * i + (u + 1))
                            for j in range(4):
                                m = nc.tensor.matmul(hidden[u][:, j * P:(j + 1) * P], w1[:, j, :], basisT[:, u, :], start=True, stop=True)
                            m.then_inc(hidden_ready, 1)
                        for u in range(2):
                            pe.wait_ge(hid_ready, 2 * i + (u + 3))
                            pe.wait_ge(stage_ready, 2 * i + (u + 1))
                            for j in range(4):
                                m = nc.tensor.matmul(factor[u][:, j * P:(j + 1) * P], hid[:, u, j * P:(j + 1) * P], w2[:, :], start=True, stop=True)
                            m.then_inc(factor_ready, 1)
                    trips(pe, body)

                @block.scalar
                def _(act):
                    prime(act, S, stored)
                    act.wait_ge(w_in, 16 * 7)

                    def body(i, tail):
                        for u in range(2):
                            act.wait_ge(hidden_ready, 2 * i + (u + 1))
                            act.wait_ge(hid_ready, 2 * i + (u + 1))
                            nc.scalar.activation(sig[:, u, :], hidden[u][:, :], ACT.Sigmoid, bias=b1c[:, 0:1]).then_inc(act_done, 1)
                            nc.scalar.activation(lin[:, u, :], hidden[u][:, :], ACT.Identity, bias=b1c[:, 0:1]).then_inc(act_done, 1)
                        for u in range(2):
                            act.wait_ge(stage_ready, 2 * i + (u + 3))
                            act.dma_start(edge_w[ds((2 * i + u) * CH, CH), :].rearrange("(t p) f -> p t f", p=P), stage[:, u, :, :]).then_inc(stored[u], 16)
                    trips(act, body)
                    for u in range(2):
                        act.wait_ge(stored[u], 16 + 16 * (NCH // 2))

                @block.vector
                def _(dve):
                    nc.vector.memset(w1[:, :, :], 0.0).then_inc(w_zero, 1)
                    dve.wait_ge(w_in, 16 * 7)
                    dve.sem_inc(basisT_ready, 2)
                    dve.sem_inc(hid_ready, 2)
                    dve.sem_inc(stage_ready, 2)

                    def body(i, tail):
                        for u in range(2):
                            dve.wait_ge(turned_ready, 2 * i + (u + 3))
                            nc.vector.tensor_copy(basisT[:, u, :], turned[u][0:4 * SW, 0:P]).then_inc(basisT_ready, 1)
                        for u in range(2):
                            dve.wait_ge(act_done, 4 * i + 2 * (u + 1))
                            nc.vector.tensor_tensor(hid[:, u, :], sig[:, u, :], lin[:, u, :], ALU.mult).then_inc(hid_ready, 1)
                        for u in range(2):
                            dve.wait_ge(factor_ready, 2 * i + (u + 1))
                            dve.wait_ge(stored[u], 16 * i + 16)
                            nc.vector.tensor_tensor(stage[:, u, :, :], factor[u][:, :].rearrange("p (t f) -> p t f", t=4),
                                                    b2r[:, :].unsqueeze(1).broadcast_to([P, 4, D]), ALU.add).then_inc(stage_ready, 1)
                    trips(dve, body)


def turn(nc, S, name, x_nm, out_fm):
    with ExitStack() as st:
        rows = st.enter_context(nc.sbuf_tensor(f"{name}_rows", [P, 2, 4, D], F32))
        stage = st.enter_context(nc.sbuf_tensor(f"{name}_stage", [P, 2, CH], F32))
        turned = [st.enter_context(nc.psum_tensor(f"{name}_turned{u}", [P, 512], F32)) for u in range(2)]
        with Phase(nc, "in0", "in1", "turned_ready", "stage_ready", "stored0", "stored1") as (
                in0, in1, turned_ready, stage_ready, stored0, stored1):
            loaded, stored = [in0, in1], [stored0, stored1]
            with nc.Block() as block:
                @block.sync
                def _(sp):
                    def body(i, tail):
                        for u in range(2):
                            sp.wait_ge(turned_ready, 2 * i + (u + 1))
                            sp.dma_start(rows[:, u, :, :], x_nm[ds((2 * i + u) * CH, CH), :].rearrange("(t p) f -> p t f", p=P)).then_inc(loaded[u], 16)
                    trips(sp, body)

                @block.tensor
                def _(pe):
                    pe.sem_inc(turned_ready, 2)

                    def body(i, tail):
                        for u in range(2):
                            pe.wait_ge(loaded[u], 16 * i + 16)
                            pe.wait_ge(stage_ready, 2 * i + (u + 1))
                            for j in range(4):
                                m = nc.tensor.transpose(turned[u][:, j * P:(j + 1) * P], rows[:, u, j, :], S.ident[:, :])
                            m.then_inc(turned_ready, 1)
                    trips(pe, body)

                @block.scalar
                def _(act):
                    prime(act, S, stored)
                    act.sem_inc(stage_ready, 2)

                    def body(i, tail):
                        for u in range(2):
                            act.wait_ge(turned_ready, 2 * i + (u + 3))
                            act.wait_ge(stored[u], 16 * i + 16)
                            nc.scalar.copy(stage[:, u, :], turned[u][:, :]).then_inc(stage_ready, 1)
                            act.wait_ge(stage_ready, 2 * i + (u + 3))
                            act.dma_start(out_fm[:, ds((2 * i + u) * CH, CH)], stage[:, u, :]).then_inc(stored[u], 16)
                    trips(act, body)
                    for u in range(2):
                        act.wait_ge(stored[u], 16 + 16 * (NCH // 2))


def dense_fm(nc, S, name, ins, bias, func, out_fm, stats=None):
    K = len(ins)
    pre_k = [n for n, x in enumerate(ins) if len(x) > 2]
    with ExitStack() as st:
        sb = lambda n, s, d=F32: st.enter_context(nc.sbuf_tensor(f"{name}_{n}", s, d))
        raw = sb("raw", [P, 2, K, CH])
        pre = sb("pre", [P, 2, CH]) if pre_k else None
        stage = sb("stage", [P, 2, CH])
        st6 = sb("st6", [P, NCH, 6]) if stats else None
        mv = sb("mv", [P, 4]) if stats else None
        z = [st.enter_context(nc.psum_tensor(f"{name}_z{u}", [P, 512], F32)) for u in range(2)]
        with Phase(nc, "in0", "in1", "pre_ready", "z_ready", "stage_ready", "stats_done", "passed", "chain", "root", "stored0", "stored1") as (
                in0, in1, pre_ready, z_ready, stage_ready, stats_done, passed, chain, root, stored0, stored1):
            loaded, stored = [in0, in1], [stored0, stored1]
            with nc.Block() as block:
                @block.sync
                def _(sp):
                    def body(i, tail):
                        for u in range(2):
                            sp.wait_ge(z_ready, 2 * i + (u + 1))
                            for n, x in enumerate(ins):
                                sp.dma_start(raw[:, u, n, :], x[0][:, ds((2 * i + u) * CH, CH)]).then_inc(loaded[u], 16)
                    trips(sp, body)

                @block.tensor
                def _(pe):
                    pe.sem_inc(z_ready, 2)

                    def body(i, tail):
                        for u in range(2):
                            pe.wait_ge(loaded[u], 16 * K * (i + 1))
                            if pre_k:
                                pe.wait_ge(pre_ready, 2 * i + (u + 1))
                            pe.wait_ge(stage_ready, 2 * i + (u + 1))
                            for n, x in enumerate(ins):
                                src = pre[:, u, :] if n in pre_k else raw[:, u, n, :]
                                m = nc.tensor.matmul(z[u][:, :], x[1], src, start=(n == 0), stop=(n == K - 1))
                            m.then_inc(z_ready, 1)
                    trips(pe, body)

                @block.scalar
                def _(act):
                    prime(act, S, stored)
                    act.sem_inc(stage_ready, 2)

                    def body(i, tail):
                        if pre_k:
                            for u in range(2):
                                act.wait_ge(loaded[u], 16 * K * (i + 1))
                                act.wait_ge(z_ready, 2 * i + (u + 1))
                                nc.scalar.activation(pre[:, u, :], raw[:, u, pre_k[0], :], ACT.Relu, bias=ins[pre_k[0]][3],
                                                     scale=ins[pre_k[0]][2]).then_inc(pre_ready, 1)
                        for u in range(2):
                            act.wait_ge(z_ready, 2 * i + (u + 3))
                            act.wait_ge(stored[u], 16 * i + 16)
                            if stats:
                                act.wait_ge(stats_done, 2 * i + (u + 1))
                            if bias is None:
                                ins_ = nc.scalar.activation(stage[:, u, :], z[u][:, :], func)
                            else:
                                ins_ = nc.scalar.activation(stage[:, u, :], z[u][:, :], func, bias=bias)
                            ins_.then_inc(stage_ready, 1)
                            act.wait_ge(stage_ready, 2 * i + (u + 3))
                            act.dma_start(out_fm[:, ds((2 * i + u) * CH, CH)], stage[:, u, :]).then_inc(stored[u], 16)
                    trips(act, body)
                    for u in range(2):
                        act.wait_ge(stored[u], 16 + 16 * (NCH // 2))
                    if stats:
                        act.wait_ge(chain, 3)
                        nc.scalar.activation(mv[:, 3:4], mv[:, 2:3], ACT.Sqrt).then_inc(root, 1)

                @block.vector
                def _(dve):
                    if not stats:
                        return
                    dve.sem_inc(stats_done, 2)

                    def body(i, tail):
                        for u in range(2):
                            dve.wait_ge(stage_ready, 2 * i + (u + 3))
                            gate(dve, passed)
                            nc.vector.bn_stats(st6[:, ds(2 * i + u, 1), :].rearrange("p a b -> p (a b)"), stage[:, u, :]).then_inc(stats_done, 1)
                    trips(dve, body)
                    dve.wait_ge(stats_done, 2 + NCH)
                    c = Chain(dve, chain)
                    c.link(nc.vector.bn_stats(st6[:, NCH - 1, :], stage[:, 1, 0:N - (NCH - 1) * CH]))
                    c.link(nc.vector.bn_aggr(mv[:, 0:2], st6[:, :, :].rearrange("p a b -> p (a b)")))
                    c.link(nc.vector.tensor_scalar(mv[:, 2:3], mv[:, 1:2], EPS, None, ALU.add))
                    gain, beta, scale, shift = stats
                    dve.wait_ge(root, 1)
                    c.link(nc.vector.reciprocal(mv[:, 2:3], mv[:, 3:4]))
                    c.link(nc.vector.tensor_tensor(scale, mv[:, 2:3], gain, ALU.mult))
                    c.link(nc.vector.tensor_tensor(mv[:, 3:4], scale, mv[:, 0:1], ALU.mult))
                    c.link(nc.vector.tensor_tensor(shift, beta, mv[:, 3:4], ALU.subtract))


def dense_nm(nc, S, name, in_fm, M, w, pitch, bias, out_nm, pre=None, pre_fm=None):
    with ExitStack() as st:
        sb = lambda n, s, d=F32: st.enter_context(nc.sbuf_tensor(f"{name}_{n}", s, d))
        raw = sb("raw", [P, 2, CH])
        act_in = sb("pre", [P, 2, CH]) if pre else None
        stage = sb("stage", [P, 2, 4, w])
        z = [st.enter_context(nc.psum_tensor(f"{name}_z{u}", [P, 4, pitch], F32)) for u in range(2)]
        with Phase(nc, "in0", "in1", "pre_ready", "z_ready", "stage_ready", "stored0", "stored1", "kept0", "kept1") as (
                in0, in1, pre_ready, z_ready, stage_ready, stored0, stored1, kept0, kept1):
            loaded, stored, kept = [in0, in1], [stored0, stored1], [kept0, kept1]
            with nc.Block() as block:
                @block.sync
                def _(sp):
                    def body(i, tail):
                        for u in range(2):
                            sp.wait_ge(z_ready, 2 * i + (u + 1))
                            if pre:
                                sp.wait_ge(pre_ready, 2 * i + (u + 1))
                            sp.dma_start(raw[:, u, :], in_fm[:, ds((2 * i + u) * CH, CH)]).then_inc(loaded[u], 16)
                    trips(sp, body)

                @block.tensor
                def _(pe):
                    pe.sem_inc(z_ready, 2)

                    def body(i, tail):
                        for u in range(2):
                            if pre:
                                pe.wait_ge(pre_ready, 2 * i + (u + 3))
                            else:
                                pe.wait_ge(loaded[u], 16 * i + 16)
                            pe.wait_ge(stage_ready, 2 * i + (u + 1))
                            src = act_in if pre else raw
                            for j in range(4):
                                m = nc.tensor.matmul(z[u][:, j, 0:w], src[:, u, j * P:(j + 1) * P], M, start=True, stop=True)
                            m.then_inc(z_ready, 1)
                    trips(pe, body)

                @block.scalar
                def _(act):
                    prime(act, S, stored + (kept if pre_fm is not None else []))
                    if pre:
                        act.sem_inc(pre_ready, 2)

                    def body(i, tail):
                        if pre:
                            for u in range(2):
                                act.wait_ge(loaded[u], 16 * i + 16)
                                act.wait_ge(z_ready, 2 * i + (u + 1))
                                if pre_fm is not None:
                                    act.wait_ge(kept[u], 16 * i + 16)
                                nc.scalar.activation(act_in[:, u, :], raw[:, u, :], ACT.Relu, bias=pre[1], scale=pre[0]).then_inc(pre_ready, 1)
                                if pre_fm is not None:
                                    act.wait_ge(pre_ready, 2 * i + (u + 3))
                                    act.dma_start(pre_fm[:, ds((2 * i + u) * CH, CH)], act_in[:, u, :]).then_inc(kept[u], 16)
                        for u in range(2):
                            act.wait_ge(stage_ready, 2 * i + (u + 3))
                            act.dma_start(out_nm[ds((2 * i + u) * CH, CH), :].rearrange("(t p) w -> p t w", p=P), stage[:, u, :, :]).then_inc(stored[u], 16)
                    trips(act, body)
                    for u in range(2):
                        act.wait_ge(stored[u], 16 + 16 * (NCH // 2))
                        if pre_fm is not None:
                            act.wait_ge(kept[u], 16 + 16 * (NCH // 2))

                @block.vector
                def _(dve):
                    dve.sem_inc(stage_ready, 2)

                    def body(i, tail):
                        for u in range(2):
                            dve.wait_ge(z_ready, 2 * i + (u + 3))
                            dve.wait_ge(stored[u], 16 * i + 16)
                            if bias is None:
                                ins = nc.vector.tensor_copy(stage[:, u, :, :], z[u][:, :, 0:w])
                            else:
                                ins = nc.vector.tensor_tensor(stage[:, u, :, :], z[u][:, :, 0:w],
                                                              bias.unsqueeze(1).broadcast_to([P, 4, w]), ALU.add)
                            ins.then_inc(stage_ready, 1)
                    trips(dve, body)


def residual_norm(nc, S, name, u_fm, x_nm, outs_nm, outs_fm):
    tail_out = outs_nm[0].shape[0] == N
    STEPS = 28
    NO, NF = len(outs_nm), len(outs_fm)
    with ExitStack() as st:
        sb = lambda n, s, d=F32: st.enter_context(nc.sbuf_tensor(f"{name}_{n}", s, d))
        ut = sb("ut", [P, 2, CH]); xin = sb("xin", [P, 2, 4, D]); y = sb("y", [P, 2, 4, D]); xn = sb("xn", [P, 2, 4, D])
        st6 = sb("st6", [P, 2, 4, 6]); mv = sb("mv", [P, 2, 4, 2]); rs = sb("rs", [P, 2, 2, 4]); stage = sb("stage", [P, 2, CH])
        eps = sb("eps", [P, 1])
        un = [st.enter_context(nc.psum_tensor(f"{name}_un{u}", [P, 512], F32)) for u in range(2)]
        xt = [st.enter_context(nc.psum_tensor(f"{name}_xt{u}", [P, 512], F32)) for u in range(2)]
        with Phase(nc, "in0", "in1", "eps_set", "u_turned", "dve", "passed", "rooted", "x_turned", "stage_ready", "xn_ready", "st0", "st1", "sf0", "sf1") as (
                in0, in1, eps_set, u_turned, dve_sem, passed, rooted, x_turned, stage_ready, xn_ready, st0, st1, sf0, sf1):
            loaded, stored, stored_fm = [in0, in1], [st0, st1], [sf0, sf1]
            with nc.Block() as block:
                @block.sync
                def _(sp):
                    def body(i, tail):
                        for u in range(2):
                            sp.wait_ge(xn_ready, 2 * i + (u + 1))
                            c0 = (2 * i + u) * CH
                            sp.dma_start(ut[:, u, :], u_fm[:, ds(c0, CH)]).then_inc(loaded[u], 16)
                            sp.dma_start(xin[:, u, :, :], x_nm[ds(c0, CH), :].rearrange("(t p) f -> p t f", p=P)).then_inc(loaded[u], 16)
                    trips(sp, body)

                @block.tensor
                def _(pe):
                    pe.sem_inc(x_turned, 1)

                    def body(i, tail):
                        for u in range(2):
                            pe.wait_ge(loaded[u], 32 * i + 32)
                            pe.wait_ge(xn_ready, 2 * i + (u + 1))
                            for j in range(4):
                                m = nc.tensor.transpose(un[u][:, j * P:(j + 1) * P], ut[:, u, j * P:(j + 1) * P], S.ident[:, :])
                            m.then_inc(u_turned, 1)
                        if outs_fm:
                            for u in range(2):
                                pe.wait_ge(xn_ready, 2 * i + (u + 3))
                                pe.wait_ge(stage_ready, 2 * i + (u + 1))
                                for j in range(4):
                                    m = nc.tensor.transpose(xt[u][:, j * P:(j + 1) * P], xn[:, u, j, :], S.ident[:, :])
                                m.then_inc(x_turned, 1)
                    trips(pe, body)

                @block.scalar
                def _(act):
                    prime(act, S, stored + stored_fm)
                    act.sem_inc(stage_ready, 2)
                    act.wait_ge(eps_set, 1)

                    def body(i, tail):
                        for u in range(2):
                            act.wait_ge(dve_sem, STEPS * i + 18)
                            nc.scalar.activation(rs[:, u, 0, :], mv[:, u, :, 1], ACT.Sqrt, bias=eps[:, 0:1]).then_inc(rooted, 1)
                        for u in range(2):
                            act.wait_ge(xn_ready, 2 * i + (u + 3))
                            for o in outs_nm:
                                if tail and u == 1 and tail_out:
                                    c0, full = (NCH - 1) * CH, (N - (NCH - 1) * CH) // P
                                    act.dma_start(o[c0:c0 + full * P, :].rearrange("(t p) f -> p t f", p=P), xn[:, u, 0:full, :]).then_inc(stored[u], 16)
                                    act.dma_start(o[c0 + full * P:N, :], xn[0:N - c0 - full * P, u, full, :]).then_inc(stored[u], 16)
                                else:
                                    act.dma_start(o[ds((2 * i + u) * CH, CH), :].rearrange("(t p) f -> p t f", p=P), xn[:, u, :, :]).then_inc(stored[u], 16)
                        if outs_fm:
                            for u in range(2):
                                act.wait_ge(x_turned, 2 * i + (u + 2))
                                act.wait_ge(stored_fm[u], 16 * NF * i + 16)
                                nc.scalar.copy(stage[:, u, :], xt[u][:, :]).then_inc(stage_ready, 1)
                                act.wait_ge(stage_ready, 2 * i + (u + 3))
                                for o in outs_fm:
                                    act.dma_start(o[:, ds((2 * i + u) * CH, CH)], stage[:, u, :]).then_inc(stored_fm[u], 16)
                    trips(act, body, peel=True)
                    for u in range(2):
                        act.wait_ge(stored[u], 16 + 16 * NO * (NCH // 2) + (16 if tail_out and u == 1 else 0))
                        act.wait_ge(stored_fm[u], 16 + 16 * NF * (NCH // 2))

                @block.vector
                def _(dve):
                    nc.vector.memset(eps[:, :], EPS).then_inc(eps_set, 1)
                    dve.sem_inc(xn_ready, 2)

                    def body(i, tail):
                        c = Chain(dve, dve_sem, STEPS * i)
                        for u in range(2):
                            dve.wait_ge(u_turned, 2 * i + (u + 1))
                            c.add(nc.vector.tensor_tensor(y[:, u, :, :], un[u][:, :].rearrange("p (t f) -> p t f", t=4), xin[:, u, :, :], ALU.add))
                        for u in range(2):
                            dve.wait_ge(dve_sem, STEPS * i + 2)
                            for j in range(4):
                                c.add(nc.vector.bn_stats(st6[:, u, j, :], y[:, u, j, :]))
                        dve.wait_ge(dve_sem, STEPS * i + 10)
                        gate(dve, passed)
                        for u in range(2):
                            for j in range(4):
                                c.add(nc.vector.bn_aggr(mv[:, u, j, :], st6[:, u, j, :]))
                        for u in range(2):
                            dve.wait_ge(rooted, 2 * i + (u + 1))
                            c.add(nc.vector.reciprocal(rs[:, u, 1, :], rs[:, u, 0, :]))
                        for u in range(2):
                            dve.wait_ge(dve_sem, STEPS * i + 20)
                            dve.wait_ge(stored[u], 16 * NO * i + 16)
                            if outs_fm:
                                dve.wait_ge(x_turned, 2 * i + (u + 1))
                            for j in range(4):
                                ins = nc.vector.tensor_scalar(xn[:, u, j, :], y[:, u, j, :], mv[:, u, j, 0:1], rs[:, u, 1, j:j + 1],
                                                              ALU.subtract, ALU.mult)
                                if j < 3:
                                    c.add(ins)
                                else:
                                    ins.then_inc(xn_ready, 1)
                        assert c.n == 26
                        dve.sem_inc(dve_sem, STEPS - 26)
                    trips(dve, body)


def attention_rows(nc, S, by_dst, table, wr, edge_rows):
    NI = ET // 8
    with ExitStack() as st:
        sb = lambda n, s, d=F32: st.enter_context(nc.sbuf_tensor(f"a1_{n}", s, d))
        index = sb("index", [P, 2, 2, 4], I32)
        src_rows = sb("src_rows", [P, 2, 4, DW]); dst_rows = sb("dst_rows", [P, 2, 4, DW])
        attr = sb("attr", [P, 2, 4, D]); attrT = sb("attrT", [P, 2, CH]); msg = sb("msg", [P, 2, 4, DW]); lg = sb("lg", [P, 2, 4])
        turned = [st.enter_context(nc.psum_tensor(f"a1_turned{u}", [P, 512], F32)) for u in range(2)]
        rel = [st.enter_context(nc.psum_tensor(f"a1_rel{u}", [P, 4, 256], F32)) for u in range(2)]
        with Phase(nc, "g0", "g1", "in0", "in1", "index_ready", "pool_go", "turned_ready", "attrT_ready", "rel_ready",
                   "msg_ready", "dve_sem", "logit_ready", "st0", "st1") as (
                g0, g1, in0, in1, index_ready, pool_go, turned_ready, attrT_ready, rel_ready, msg_ready, dve_sem, logit_ready, st0, st1):
            gathered, loaded, stored = [g0, g1], [in0, in1], [st0, st1]
            with nc.Block() as block:
                @block.sync
                def _(sp):
                    with sp.Fori(0, NI) as i:
                        for h in range(2):
                            sp.wait_ge(turned_ready, 2 * i + (h + 1))
                            sp.dma_start(attr[:, h, :, :], by_dst[ds((2 * i + h) * CH, CH), 0:D].rearrange("(t p) w -> p t w", p=P)).then_inc(loaded[h], 16)

                @block.gpsimd
                def _(pool):
                    with pool.Fori(0, NI) as i:
                        for h in range(2):
                            pool.wait_ge(index_ready, 4 * i + 2 * (h + 1))
                            pool.wait_ge(logit_ready, 2 * i + (h + 1))
                            nc.gpsimd.sem_inc(pool_go, 1)
                            for j in range(4):
                                for e, rows in enumerate((src_rows, dst_rows)):
                                    nc.gpsimd.indirect_dma_start(rows[:, h, j, :], None, table[:, :],
                                                                 bass.IndirectOffsetOnAxis(ap=index[:, h, e, j:j + 1], axis=0)).then_inc(gathered[h], 16)
                    for h in range(2):
                        pool.wait_ge(gathered[h], 128 * NI)

                @block.tensor
                def _(pe):
                    pe.sem_inc(turned_ready, 2)
                    with pe.Fori(0, NI) as i:
                        for h in range(2):
                            pe.wait_ge(loaded[h], 16 * i + 16)
                            pe.wait_ge(attrT_ready, 2 * i + (h + 1))
                            for j in range(4):
                                m = nc.tensor.transpose(turned[h][:, j * P:(j + 1) * P], attr[:, h, j, :], S.ident[:, :])
                            m.then_inc(turned_ready, 1)
                        for h in range(2):
                            pe.wait_ge(attrT_ready, 2 * i + (h + 3))
                            pe.wait_ge(msg_ready, 2 * i + (h + 1))
                            for j in range(4):
                                m = nc.tensor.matmul(rel[h][:, j, 0:DW], attrT[:, h, j * P:(j + 1) * P], wr, start=True, stop=True)
                            m.then_inc(rel_ready, 1)

                @block.scalar
                def _(act):
                    prime(act, S, stored)
                    act.sem_inc(attrT_ready, 2)
                    with act.Fori(0, NI) as i:
                        for h in range(2):
                            act.wait_ge(turned_ready, 2 * i + (h + 3))
                            nc.scalar.copy(attrT[:, h, :], turned[h][:, :]).then_inc(attrT_ready, 1)
                        for h in range(2):
                            act.wait_ge(msg_ready, 2 * i + (h + 3))
                            act.dma_start(edge_rows[ds((2 * i + h) * CH, CH), :].rearrange("(t p) w -> p t w", p=P), msg[:, h, :, 0:D]).then_inc(stored[h], 16)
                    for h in range(2):
                        act.wait_ge(stored[h], 16 + 16 * NI)

                @block.vector
                def _(dve):
                    dve.sem_inc(msg_ready, 2)
                    dve.sem_inc(logit_ready, 2)
                    with dve.Fori(0, NI) as i:
                        for h in range(2):
                            t = 8 * i + 4 * h
                            nc.vector.tensor_copy(index[:, h, 0, :], S.other[1][:, ds(t, 4)]).then_inc(index_ready, 1)
                            nc.vector.tensor_copy(index[:, h, 1, :], S.keyi[1][:, ds(t, 4)]).then_inc(index_ready, 1)
                        for h in range(2):
                            t = 8 * i + 4 * h
                            dve.wait_ge(gathered[h], 128 * i + 128)
                            dve.wait_ge(rel_ready, 2 * i + (h + 1))
                            dve.wait_ge(stored[h], 16 * i + 16)
                            nc.vector.tensor_tensor(msg[:, h, :, 0:D + 1], rel[h][:, :, 0:D + 1], src_rows[:, h, :, 0:D + 1], ALU.add).then_inc(msg_ready, 1)
                            dve.wait_ge(msg_ready, 2 * i + (h + 3))
                            nc.vector.tensor_tensor(lg[:, h, :], msg[:, h, :, D], dst_rows[:, h, :, D + 1], ALU.add).then_inc(dve_sem, 1)
                            dve.wait_ge(dve_sem, 2 * i + (h + 1))
                            nc.vector.scalar_tensor_tensor(S.logit[:, ds(t, 4)], lg[:, h, :], 0.01, lg[:, h, :], ALU.mult, ALU.max).then_inc(logit_ready, 1)


def head_logits(nc, S, q_nm, kv_nm, edge_rows):
    NI = ET // 8
    with ExitStack() as st:
        sb = lambda n, s, d=F32: st.enter_context(nc.sbuf_tensor(f"a2_{n}", s, d))
        index = sb("index", [P, 2, 2, 4], I32)
        qr = sb("qr", [P, 2, 4, D]); kv = sb("kv", [P, 2, 4, 2 * D]); prod = sb("prod", [P, 2, 4, D])
        with Phase(nc, "g0", "g1", "index_ready", "pool_go", "prod_ready", "logit_ready", "st0", "st1") as (
                g0, g1, index_ready, pool_go, prod_ready, logit_ready, st0, st1):
            gathered, stored = [g0, g1], [st0, st1]
            with nc.Block() as block:
                @block.gpsimd
                def _(pool):
                    with pool.Fori(0, NI) as i:
                        for h in range(2):
                            pool.wait_ge(index_ready, 4 * i + 2 * (h + 1))
                            pool.wait_ge(prod_ready, 2 * i + (h + 1))
                            pool.wait_ge(stored[h], 16 * i + 16)
                            nc.gpsimd.sem_inc(pool_go, 1)
                            for j in range(4):
                                nc.gpsimd.indirect_dma_start(qr[:, h, j, :], None, q_nm[:, :],
                                                             bass.IndirectOffsetOnAxis(ap=index[:, h, 0, j:j + 1], axis=0)).then_inc(gathered[h], 16)
                                nc.gpsimd.indirect_dma_start(kv[:, h, j, :], None, kv_nm[:, :],
                                                             bass.IndirectOffsetOnAxis(ap=index[:, h, 1, j:j + 1], axis=0)).then_inc(gathered[h], 16)
                    for h in range(2):
                        pool.wait_ge(gathered[h], 128 * NI)

                @block.scalar
                def _(act):
                    prime(act, S, stored)
                    with act.Fori(0, NI) as i:
                        for h in range(2):
                            act.wait_ge(gathered[h], 128 * i + 128)
                            act.dma_start(edge_rows[ds((2 * i + h) * CH, CH), :].rearrange("(t p) w -> p t w", p=P), kv[:, h, :, D:2 * D]).then_inc(stored[h], 16)
                    for h in range(2):
                        act.wait_ge(stored[h], 16 + 16 * NI)

                @block.vector
                def _(dve):
                    dve.sem_inc(prod_ready, 2)
                    dve.sem_inc(logit_ready, 2)
                    with dve.Fori(0, NI) as i:
                        for h in range(2):
                            t = 8 * i + 4 * h
                            nc.vector.tensor_copy(index[:, h, 0, :], S.keyi[0][:, ds(t, 4)]).then_inc(index_ready, 1)
                            nc.vector.tensor_copy(index[:, h, 1, :], S.other[0][:, ds(t, 4)]).then_inc(index_ready, 1)
                        for h in range(2):
                            t = 8 * i + 4 * h
                            dve.wait_ge(gathered[h], 128 * i + 128)
                            dve.wait_ge(logit_ready, 2 * i + (h + 1))
                            nc.vector.tensor_tensor(prod[:, h, :, :], qr[:, h, :, :], kv[:, h, :, 0:D], ALU.mult).then_inc(prod_ready, 1)
                            dve.wait_ge(prod_ready, 2 * i + (h + 3))
                            gate(dve, pool_go)
                            nc.vector.tensor_reduce(S.logit[:, ds(t * HEADS, 4 * HEADS)].rearrange("p (t h) -> p t h", h=HEADS),
                                                    prod[:, h, :, :].rearrange("p t (d h) -> p t h d", h=HEADS),
                                                    mybir.AxisListType.X, ALU.add).then_inc(logit_ready, 1)


R = ET // 4
BIG = 1.0e30


def segment_links(nc, S, name, k):
    with ExitStack() as st:
        sb = lambda n, s: st.enter_context(nc.sbuf_tensor(f"{name}_{n}", s, F32))
        ps = lambda n: st.enter_context(nc.psum_tensor(f"{name}_{n}", [P, 512], F32))
        down, up, keys, col = sb("down", [P, R]), sb("up", [P, R]), sb("keys", [R, CH]), sb("col", [R, 4])
        wide, small = ps("wide"), ps("small")
        with Phase(nc, "pe_done", "chain") as (pe_done, chain):
            with nc.Block() as block:
                @block.tensor
                def _(pe):
                    for j in range(4):
                        m = nc.tensor.transpose(wide[0:R, j * P:(j + 1) * P],
                                                S.key[k][:, :].rearrange("p (r j) -> p j r", j=4)[:, j, :], S.ident[:, :])
                    m.then_inc(pe_done, 1)
                    pe.wait_ge(chain, 3)
                    nc.tensor.matmul(small[0:R, 0:1], down[0:R, :], keys[:, CH - 1:CH], start=True, stop=True).then_inc(pe_done, 1)
                    pe.wait_ge(chain, 7)
                    nc.tensor.matmul(small[0:R, 1:2], up[0:R, :], S.link[0][:, 0:1], start=True, stop=True).then_inc(pe_done, 1)
                    pe.wait_ge(chain, 13)
                    for d in range(2):
                        m = nc.tensor.matmul(small[0:1, P * (d + 1):P * (d + 1) + R], col[:, 2 + d:3 + d], S.ident[0:R, 0:R], start=True, stop=True)
                    m.then_inc(pe_done, 1)

                @block.vector
                def _(dve):
                    c = Chain(dve, chain)
                    c.add(nc.vector.tensor_scalar(down[:, :], S.iota_row[:, 0:R], -1.0, S.iota_col[:, 0:1], ALU.add, ALU.is_equal))
                    c.add(nc.vector.tensor_scalar(up[:, :], S.iota_row[:, 0:R], 1.0, S.iota_col[:, 0:1], ALU.add, ALU.is_equal))
                    dve.wait_ge(pe_done, 1)
                    c.link(nc.vector.tensor_copy(keys[:, :], wide[0:R, :]))
                    c.link(nc.vector.tensor_scalar(col[:, 0:1], S.iota_col[0:R, 0:1], 0.0, None, ALU.is_equal))
                    dve.wait_ge(pe_done, 2)
                    c.link(nc.vector.tensor_tensor(col[:, 1:2], small[0:R, 0:1], col[:, 0:1], ALU.subtract))
                    c.link(nc.vector.tensor_tensor(S.link[0][:, 1:CH], keys[:, 1:CH], keys[:, 0:CH - 1], ALU.is_equal))
                    c.link(nc.vector.tensor_tensor(S.link[0][:, 0:1], keys[:, 0:1], col[:, 1:2], ALU.is_equal))
                    c.link(nc.vector.tensor_copy(S.link[1][:, 0:CH - 1], S.link[0][:, 1:CH]))
                    dve.wait_ge(pe_done, 3)
                    c.link(nc.vector.tensor_copy(S.link[1][:, CH - 1:CH], small[0:R, 1:2]))
                    for d in range(2):
                        c.link(nc.vector.tensor_scalar(S.open[d][:, :], S.link[d][:, :], -1.0, BIG, ALU.add, ALU.mult))
                        c.link(nc.vector.tensor_reduce(col[:, 2 + d:3 + d], S.link[d][:, :], mybir.AxisListType.X, ALU.min))
                    dve.wait_ge(pe_done, 4)
                    for d in range(2):
                        c.link(nc.vector.tensor_copy(S.row_link[d][:, :], small[0:1, P * (d + 1):P * (d + 1) + R]))
                        c.link(nc.vector.tensor_scalar(S.row_open[d][:, :], S.row_link[d][:, :], -1.0, BIG, ALU.add, ALU.mult))


SCANS = [(0, 0), (1, 0), (0, 1), (1, 0)]


def segment_softmax(nc, S, name, heads, factor):
    PER = 28
    PES = 10
    AT = [2, 7, 13, 18]
    with ExitStack() as st:
        sb = lambda n, s: st.enter_context(nc.sbuf_tensor(f"{name}_{n}", s, F32))
        ps = lambda n: st.enter_context(nc.psum_tensor(f"{name}_{n}", [P, 512], F32))
        head = sb("head", [P, ET])
        v = [sb(f"v{n}", [R, CH]) for n in range(6)]
        first = sb("first", [R, CH]); ex = sb("ex", [R, CH])
        lastrow, states, carry = sb("lastrow", [1, R]), sb("states", [1, 4, R + 2]), sb("carry", [R, 4])
        wide, small, back = ps("wide"), ps("small"), ps("back")
        src = [v[0], v[1], ex, v[4]]
        dst = [v[1], v[2], v[4], v[5]]
        logit = S.logit[:, 0:ET * heads].rearrange("p (t h) -> p t h", h=heads)
        alpha = S.logit[:, 0:ET * heads].rearrange("p (r j h) -> p j r h", h=heads, j=4)
        with Phase(nc, "borders_set", "pe_done", "chain", "exp_done") as (borders_set, pe_done, chain, exp_done):
            with nc.Block() as block:
                @block.tensor
                def _(pe):
                    with pe.Fori(0, heads) as g:
                        pe.wait_ge(chain, PER * g + 1)
                        for j in range(4):
                            m = nc.tensor.transpose(wide[0:R, j * P:(j + 1) * P],
                                                    head[:, :].rearrange("p (r j) -> p j r", j=4)[:, j, :], S.ident[:, :])
                        m.then_inc(pe_done, 1)
                        for s, (backwards, _sum) in enumerate(SCANS):
                            end = 0 if backwards else CH - 1
                            pe.wait_ge(chain, PER * g + AT[s] + 1)
                            nc.tensor.matmul(small[0:1, 0:R], first[:, end:end + 1], S.ident[0:R, 0:R], start=True, stop=True).then_inc(pe_done, 1)
                            pe.wait_ge(chain, PER * g + AT[s] + 3)
                            nc.tensor.matmul(small[0:R, P + s:P + s + 1], states[0:1, s, 2 * backwards:2 * backwards + R],
                                             S.ones[0:1, 0:1], start=True, stop=True).then_inc(pe_done, 1)
                        pe.wait_ge(chain, PER * g + 25)
                        for j in range(4):
                            m = nc.tensor.transpose(back[:, j * P:j * P + R], v[0][:, j * P:(j + 1) * P], S.ident[0:R, 0:R])
                        m.then_inc(pe_done, 1)

                @block.scalar
                def _(act):
                    with act.Fori(0, heads) as g:
                        act.wait_ge(chain, PER * g + 13)
                        nc.scalar.activation(ex[:, :], v[3][:, :], ACT.Exp).then_inc(exp_done, 1)

                @block.vector
                def _(dve):
                    nc.vector.memset(states[:, :, :], -BIG).then_inc(borders_set, 1)
                    dve.wait_ge(borders_set, 1)
                    nc.vector.memset(states[:, 2, :], 0.0).then_inc(borders_set, 1)
                    dve.wait_ge(borders_set, 2)
                    with dve.Fori(0, heads) as g:
                        c = Chain(dve, chain, PER * g)
                        c.link(nc.vector.tensor_scalar(head[:, :], logit[:, :, ds(g, 1)].rearrange("p t o -> p (t o)"), factor, None, ALU.mult))
                        dve.wait_ge(pe_done, PES * g + 1)
                        c.link(nc.vector.tensor_copy(v[0][:, :], wide[0:R, :]))
                        for s, (backwards, summed) in enumerate(SCANS):
                            if s == 2:
                                c.link(nc.vector.tensor_tensor(v[3][:, :], v[0][:, :], v[2][:, :], ALU.subtract))
                                dve.wait_ge(exp_done, g + 1)
                            assert c.n == AT[s]
                            way = slice(None, None, -1) if backwards else slice(None)
                            flags, rows = (S.link, S.row_link) if summed else (S.open, S.row_open)
                            ops = (ALU.mult, ALU.add) if summed else (ALU.add, ALU.max)
                            c.link(nc.vector.tensor_tensor_scan(first[:, way], flags[backwards][:, way], src[s][:, way],
                                                                0.0 if summed else -BIG, *ops))
                            dve.wait_ge(pe_done, PES * g + 2 * s + 2)
                            c.link(nc.vector.tensor_copy(lastrow[:, :], small[0:1, 0:R]))
                            c.link(nc.vector.tensor_tensor_scan(states[:, s, 1:R + 1][:, way], rows[backwards][:, way], lastrow[:, way],
                                                                0.0 if summed else -BIG, *ops))
                            dve.wait_ge(pe_done, PES * g + 2 * s + 3)
                            c.link(nc.vector.tensor_copy(carry[:, s:s + 1], small[0:R, P + s:P + s + 1]))
                            c.link(nc.vector.tensor_tensor_scan(dst[s][:, way], flags[backwards][:, way], src[s][:, way],
                                                                carry[:, s:s + 1], *ops))
                        c.link(nc.vector.reciprocal(v[5][:, :], v[5][:, :]))
                        c.link(nc.vector.tensor_tensor(v[0][:, :], ex[:, :], v[5][:, :], ALU.mult))
                        assert c.n == 25
                        dve.wait_ge(pe_done, PES * g + 10)
                        c.link(nc.vector.tensor_scalar(alpha[:, :, :, ds(g, 1)].rearrange("p j r o -> p j (r o)"),
                                                       back[:, :].rearrange("p (j r) -> p j r", j=4)[:, :, 0:R], 1.0, None, ALU.mult))
                        dve.sem_inc(chain, PER - c.n)



def product_of(nc, S, name, out, A, B, bias=None):
    n = B.shape[1]
    with ExitStack() as st:
        t = st.enter_context(nc.psum_tensor(f"{name}_t", [P, P], F32))
        r = st.enter_context(nc.psum_tensor(f"{name}_r", [P, 512], F32))
        at = st.enter_context(nc.sbuf_tensor(f"{name}_at", [P, P], F32))
        with Phase(nc, "pe_done", "chain") as (pe_done, chain):
            with nc.Block() as block:
                @block.tensor
                def _(pe):
                    nc.tensor.transpose(t[:, :], A, S.ident[:, :]).then_inc(pe_done, 1)
                    if B is not None:
                        pe.wait_ge(chain, 1)
                        nc.tensor.matmul(r[:, 0:n], at[:, :], B, start=True, stop=True).then_inc(pe_done, 1)

                @block.vector
                def _(dve):
                    dve.wait_ge(pe_done, 1)
                    nc.vector.tensor_copy(at[:, :], t[:, :]).then_inc(chain, 1)
                    dve.wait_ge(pe_done, 2)
                    nc.vector.tensor_copy(out, r[:, 0:n])


def transposed(nc, S, name, out, A):
    with ExitStack() as st:
        t = st.enter_context(nc.psum_tensor(f"{name}_t", [P, P], F32))
        with Phase(nc, "pe_done") as (pe_done,):
            with nc.Block() as block:
                @block.tensor
                def _(pe):
                    nc.tensor.transpose(t[:, :], A, S.ident[:, :]).then_inc(pe_done, 1)

                @block.vector
                def _(dve):
                    dve.wait_ge(pe_done, 1)
                    nc.vector.tensor_copy(out, t[:, :])


def load(nc, pairs):
    with Phase(nc, "loaded") as (loaded,):
        with nc.Block() as block:
            @block.sync
            def _(sp):
                for to, of in pairs:
                    sp.dma_start(to, of).then_inc(loaded, 16)
                sp.wait_ge(loaded, 16 * len(pairs))


def column(v):
    return v.rearrange("(p o) -> p o", o=1)


def combine(nc, terms):
    with Phase(nc, "chain") as (chain,):
        with nc.Block() as block:
            @block.vector
            def _(dve):
                c = Chain(dve, chain)
                for o, x, y, op in terms:
                    if isinstance(y, float) or y.shape[1] == 1 and x.shape[1] > 1:
                        c.link(nc.vector.tensor_scalar(o, x, y, None, op))
                    else:
                        c.link(nc.vector.tensor_tensor(o, x, y, op))


class Store:
    pass


def gnn(nc, A, out):
    st = ExitStack()
    S = Store()

    def sb(name, shape, dt=F32):
        return st.enter_context(nc.sbuf_tensor(name, shape, dt))

    def dram(name, shape):
        return nc.dram_tensor(name, tuple(shape), F32, kind="Internal").ap()

    with st:
        S.iota_row = sb("iota_row", [P, HI])
        S.iota_col = sb("iota_col", [P, 1])
        S.ident = sb("ident", [P, P])
        S.earlier = sb("earlier", [P, P])
        S.later = sb("later", [P, P])
        S.ones = sb("ones", [P, 512])
        S.zeros_bf = sb("zeros_bf", [P, 512], BF16)
        S.group_base = sb("group_base", [P, SUP])
        S.key = [sb(f"key{k}", [P, ET]) for k in range(2)]
        S.other = [sb(f"other{k}", [P, ET]) for k in range(2)]
        S.keyi = [sb(f"keyi{k}", [P, ET], I32) for k in range(2)]
        S.last = [sb(f"last{k}", [P, ET + 1], I32) for k in range(2)]
        S.gidx = S.other
        S.scratch = nc.dram_tensor("scratch", (16, 16), F32, kind="Internal").ap()
        sort_st = ExitStack()
        with sort_st:
            def tmp(name, shape, dt=F32):
                return sort_st.enter_context(nc.sbuf_tensor(name, shape, dt))
            S.key_i = tmp("key_i", [P, 2, OT], I32)
            S.part_i = tmp("part_i", [P, 2, OT], I32)
            S.key_f = tmp("key_f", [P, 2, OT])
            S.key_hi = tmp("key_hi", [P, 2, OT])
            S.key_lo = tmp("key_lo", [P, 2, OT])
            S.oh_hi = tmp("oh_hi", [P, 2, HI], BF16)
            S.oh_lo = tmp("oh_lo", [P, 2, P], BF16)
            S.ohT_lo = tmp("ohT_lo", [P, 2, P])
            S.hist = tmp("hist", [P, HI])
            S.start = tmp("start", [P, HI])
            S.t392 = tmp("t392", [P, 2, HI])
            S.table = tmp("table", [P, 2, HI])
            S.junk = tmp("junk", [P, 4, HI])
            S.base = tmp("base", [P, OT])
            S.rank = tmp("rank", [P, OT])
            S.pos = tmp("pos", [P, 2, OT])
            S.cols = tmp("cols", [P, 2, 2])
            
            setup_constants(nc, S)
            load_keys(nc, S, A["src"], A["dst"])
            for k in range(2):
                count_keys(nc, S, k)
                start_offsets(nc, S, k)
                rank_keys(nc, S, k)
            by_src = dram("by_src", [EP, SW])
            by_dst = dram("by_dst", [EP, DW])
            rbf = A["edge_attr_8"].rearrange("(p t) c -> p t c", p=OP)
            attr = A["edge_attr_128"].rearrange("(p t) c -> p t c", p=OP)
            x_pad = dram("x_pad", [EP, D])
            pad_nodes(nc, S, A["x"], x_pad)
            scatter_rows(nc, S, 0, SW, lambda b, U: rbf[:, ds(b * U, U), :], by_src)
            scatter_rows(nc, S, 1, DW, lambda b, U: attr[:, ds(b * U, U), :], by_dst)

        with ExitStack() as tmps:
            S.ends = tmps.enter_context(nc.sbuf_tensor("ends", [P, ET, 2], F32))
            S.tile_f = tmps.enter_context(nc.sbuf_tensor("tile_f", [P, ET], F32))
            S.tile_i = tmps.enter_context(nc.sbuf_tensor("tile_i", [P, ET], I32))
            sorted_keys(nc, S, 0, by_src, 8)
            sorted_keys(nc, S, 1, by_dst, D)
        fm = lambda name: dram(name, [P, EP])
        nm = lambda name, w=D: dram(name, [EP, w])
        S.logit = sb("logit", [P, ET * HEADS])
        S.link = [sb(f"link{d}", [R, CH]) for d in range(2)]; S.open = [sb(f"open{d}", [R, CH]) for d in range(2)]
        S.row_link = [sb(f"row_link{d}", [1, R]) for d in range(2)]; S.row_open = [sb(f"row_open{d}", [1, R]) for d in range(2)]
        wa, wb, wc, wd, we = (sb(f"w{n}", [P, 2 * D]) for n in "abcde")
        cols = sb("cols_w", [P, 16]); bias_row = sb("bias_row", [P, 3 * D])
        c = lambda n: cols[:, n:n + 1]
        agg, u_fm, x_fm, edge_rows = fm("agg"), fm("u_fm"), fm("x_fm"), nm("edge_rows")
        x1, x2, x3, h_nm, h_fm, z1, z2 = nm("x1"), nm("x2"), nm("x3"), nm("h_nm"), fm("h_fm"), fm("z1"), fm("z2")
        table, q_nm, kv_nm = nm("hh_table", DW), nm("q_nm"), nm("kv_nm", 2 * D)
        turn(nc, S, "tx", x_pad, x_fm)

        filter_rows(nc, S, by_src, A["L0_gnn_W1"], A["L0_gnn_b1"], A["L0_gnn_W2"], A["L0_gnn_b2"], edge_rows)
        aggregate(nc, S, "g0", 0, agg, gather=x_pad, dense=edge_rows)
        load(nc, [(wa[:, 0:D], A["L0_gnn_Wcat"][0:D, :]), (wa[:, D:], A["L0_gnn_Wcat"][D:, :]), (wb[:, 0:D], A["L0_gnn_Wself"]),
                  (c(0), column(A["L0_gnn_bself"])), (c(1), column(A["L0_gnn_bcat"]))])
        product_of(nc, S, "p0", wc[:, 0:D], wb[:, 0:D], wa[:, 0:D])
        transposed(nc, S, "p1", wb[:, 0:D], wa[:, 0:D])
        product_of(nc, S, "p2", c(2), wb[:, 0:D], c(0))
        combine(nc, [(c(3), c(2), c(1), ALU.add)])
        dense_fm(nc, S, "d0", [(agg, wa[:, D:]), (x_fm, wc[:, 0:D])], c(3), ACT.Identity, u_fm)
        residual_norm(nc, S, "n0", u_fm, x_pad, [x1], [h_fm])

        segment_links(nc, S, "s1", 1)
        with nc.Fori(0, 2) as l:
            att = A["L1_gnn_Att"]
            at = lambda n: att[ds(l, 1), n * D:(n + 1) * D].rearrange("o p -> p o")
            load(nc, [(wa[:, 0:D], A["L1_gnn_W"][ds(l, 1), :, :].rearrange("o k m -> (o k) m")),
                      (wb[:, 0:D], A["L1_gnn_Wr"][ds(l, 1), :, :].rearrange("o k m -> (o k) m")),
                      (wc[:, 0:D], A["L1_gnn_Loop"][ds(l, 1), :, :].rearrange("o k m -> (o k) m")),
                      (c(0), at(0)), (c(1), at(1)), (c(2), at(2))])
            product_of(nc, S, "q0", wa[:, D:D + 2], wa[:, 0:D], cols[:, 0:2])
            product_of(nc, S, "q1", wb[:, D:D + 1], wb[:, 0:D], c(2))
            product_of(nc, S, "q2", wd[:, 0:D], wa[:, 0:D], wc[:, 0:D])
            combine(nc, [(wa[:, D + 2:DW], S.ones[:, 0:2], 0.0, ALU.mult), (wb[:, D + 1:DW], S.ones[:, 0:3], 0.0, ALU.mult)])
            dense_nm(nc, S, "t1", h_fm, wa[:, 0:DW], DW, 256, None, table)
            attention_rows(nc, S, by_dst, table, wb[:, 0:DW], edge_rows)
            segment_softmax(nc, S, "m1", 1, 1.0)
            aggregate(nc, S, "g1", 1, agg, dense=edge_rows, weights=S.logit, heads=1)
            dense_fm(nc, S, "d1", [(agg, S.ident[:, :]), (h_fm, wd[:, 0:D])], None, ACT.Relu, h_fm)
        residual_norm(nc, S, "n1", h_fm, x1, [x2], [x_fm])

        load(nc, [(wa[:, 0:D], A["L2_gnn_Wq"]), (wb[:, 0:D], A["L2_gnn_Wk"]), (wb[:, D:], A["L2_gnn_Wv"]), (wc[:, 0:D], A["L2_gnn_Wo"]),
                  (c(0), column(A["L2_gnn_bo"]))]
             + [(bias_row[:, n * D:(n + 1) * D], A[f"L2_gnn_b{x}"].rearrange("(o f) -> o f", o=1).broadcast_to([P, D])) for n, x in enumerate("qkv")])
        transposed(nc, S, "r0", wa[:, D:], wa[:, 0:D])
        transposed(nc, S, "r1", wd[:, 0:D], wb[:, 0:D])
        transposed(nc, S, "r2", wd[:, D:], wb[:, D:])
        transposed(nc, S, "r3", wc[:, D:], wc[:, 0:D])
        dense_nm(nc, S, "t2", x_fm, wa[:, D:], D, D, bias_row[:, 0:D], q_nm)
        dense_nm(nc, S, "t3", x_fm, wd[:, :], 2 * D, 256, bias_row[:, D:], kv_nm)
        head_logits(nc, S, q_nm, kv_nm, edge_rows)
        segment_links(nc, S, "s2", 0)
        segment_softmax(nc, S, "m2", HEADS, (D // HEADS) ** -0.5)
        aggregate(nc, S, "g2", 0, agg, dense=edge_rows, weights=S.logit, heads=HEADS)
        dense_fm(nc, S, "d2", [(agg, wc[:, D:])], c(0), ACT.Identity, u_fm)
        residual_norm(nc, S, "n2", u_fm, x2, [x3, h_nm], [h_fm])

        load(nc, [(bias_row[0:1, 0:5], A["L3_gnn_eps"].rearrange("(o f) -> o f", o=1)),
                  (bias_row[:, 8:13], A["L3_gnn_eps"].rearrange("(o f) -> o f", o=1).broadcast_to([P, 5]))])
        with nc.Fori(0, 5) as l:
            row = lambda x: A[f"L3_gnn_{x}"][ds(l, 1), :].rearrange("o p -> p o")
            load(nc, [(wa[:, 0:D], A["L3_gnn_W1"][ds(l, 1), :, :].rearrange("o k m -> (o k) m")),
                      (wb[:, 0:D], A["L3_gnn_W2"][ds(l, 1), :, :].rearrange("o k m -> (o k) m")),
                      (c(10), A["L3_gnn_eps"][ds(l, 1)].rearrange("(o f) -> o f", o=1).broadcast_to([P, 1]))]
                 + [(c(n), row(x)) for n, x in enumerate(["b1", "b2", "g1", "beta1", "g2", "beta2"])])
            combine(nc, [(c(11), c(10), 1.0, ALU.add), (wa[:, D:], wa[:, 0:D], c(11), ALU.mult)])
            aggregate(nc, S, "g3", 0, agg, gather=h_nm)
            dense_fm(nc, S, "d3", [(agg, wa[:, 0:D]), (h_fm, wa[:, D:])], c(0), ACT.Identity, z1, stats=(c(2), c(3), c(6), c(7)))
            dense_fm(nc, S, "d4", [(z1, wb[:, 0:D], c(6), c(7))], c(1), ACT.Identity, z2, stats=(c(4), c(5), c(8), c(9)))
            dense_nm(nc, S, "t4", z2, S.ident[:, :], D, D, None, h_nm, pre=(c(8), c(9)), pre_fm=h_fm)
        residual_norm(nc, S, "n3", h_fm, x3, [out], [])


def kernel(**inputs):
    import numpy as _np
    import concourse.bacc as _bacc
    from concourse.bass_utils import run_bass_kernel_spmd as _run

    nc = _bacc.Bacc("TRN2", target_bir_lowering=False, num_devices=1)
    arrays, args = {}, {}
    for name, a in inputs.items():
        arrays[f"in_{name}"] = _np.ascontiguousarray(a)
        args[name] = nc.dram_tensor(f"in_{name}", arrays[f"in_{name}"].shape, mybir.dt.from_np(arrays[f"in_{name}"].dtype), kind="ExternalInput").ap()
    out = nc.dram_tensor("out", (N, D), F32, kind="ExternalOutput").ap()

    gnn(nc, args, out)
    r = _run(nc, [arrays], core_ids=[0])
    return r.results[0]["out"]
```
